# Optimizing a Trainium2 kernel written in Bass

```python
import numpy as np
import jax
import jax.numpy as jnp

def _softmax(x, axis=-1):
    return jax.nn.softmax(x, axis=axis)

def _gelu(x):
    return jax.nn.gelu(x, approximate=True)

def _silu(x):
    return jax.nn.silu(x)

def _sigmoid(x):
    return jax.nn.sigmoid(x)

def _layernorm(x, axis=-1, eps=1e-05):
    m = jnp.mean(x, axis=axis, keepdims=True)
    v = jnp.var(x, axis=axis, keepdims=True)
    return (x - m) / jnp.sqrt(v + eps)

def _scatter_add(tgt, idx, src, axis=0):
    return tgt.at[idx].add(src)

def _segment_sum(src, seg, n):
    return jax.ops.segment_sum(src, seg, n)
kernel_name = 'mk_xattn_seq_d2_seqx_r4_741a5c'

def setup_inputs(seed: int=0):
    np.random.seed(seed)
    _w = jnp.asarray

    def _rec_inputs():
        import jax
        import jax.numpy as jnp
        _rk = jax.random.key(seed)
        x = -0.0002928 + 1 * jax.random.normal(jax.random.fold_in(_rk, 1), (32, 128, 256), jnp.float32)
        _lenS = 128 - jax.random.randint(jax.random.fold_in(_rk, 7), (32,), 0, max(1, 128 // 4) + 1, jnp.int32)
        _lenS2 = 128 - jax.random.randint(jax.random.fold_in(_rk, 8), (32,), 0, max(1, 128 // 4) + 1, jnp.int32)
        _ctx_1024P = jax.random.normal(jax.random.fold_in(_rk, 11), (32, 16, 256), jnp.float32)
        _ctx_1024c = jax.random.dirichlet(jax.random.fold_in(_rk, 511), 0.3 * jnp.ones((16,), jnp.float32), (32, 128))
        _ctx_1024t = jnp.einsum('bsk,bkd->bsd', _ctx_1024c, _ctx_1024P)
        _ctx_1024t = _ctx_1024t * jax.lax.rsqrt(jnp.mean(jnp.square(_ctx_1024t)) + 1e-12) * 0.953939
        ctx_1024 = -1.39393e-06 + 0.999914 * (_ctx_1024t + 0.3 * jax.random.normal(jax.random.fold_in(_rk, 611), (32, 128, 256), jnp.float32))
        _validS = jnp.arange(128)[None, :] < _lenS[:, None]
        _validS2 = jnp.arange(128)[None, :] < _lenS2[:, None]
        _causal = jnp.tril(jnp.ones((128, 128), dtype=bool))
        mask_1xS2_bf0 = jnp.logical_not(jnp.ones((1, 128), dtype=bool))
        return (x, ctx_1024, mask_1xS2_bf0)
    x, ctx_1024, mask_1xS2_bf0 = _rec_inputs()

    def _L0_xattn_setup():
        import jax, jax.numpy as jnp
        import numpy as np
        NEG = -1e+32
        EPS_LN = 1e-05

        def _layer_norm(x, w, b):
            mu = jnp.mean(x, axis=-1, keepdims=True)
            var = jnp.mean((x - mu) ** 2, axis=-1, keepdims=True)
            return (x - mu) / jnp.sqrt(var + EPS_LN) * w + b

        def _forward(query, key, values, Wk, bk, Wv, bv, Wo, bo, gammas, ln1_w, ln1_b, W1, b1, W2, b2, ln2_w, ln2_b, mask):
            B, S, D = query.shape
            H = gammas.shape[0]
            dk = D // H

            def proj(x, W, b):
                return (x @ W.T + b).reshape(B, S, H, dk).transpose(0, 2, 1, 3)
            q = proj(query, Wk, bk)
            k = proj(key, Wk, bk)
            v = proj(values, Wv, bv)
            scores = jnp.einsum('bhqd,bhkd->bhqk', q, k) / np.sqrt(dk).astype(np.float32)
            allow = jnp.tril(jnp.ones((S, S), bool), k=mask - 1)[None, None]
            scores_ = jax.nn.softmax(jnp.where(allow, scores, NEG), axis=-1)
            scores_ = scores_ * allow.astype(scores_.dtype)
            distcum = jnp.cumsum(scores_, axis=-1)
            disttotal = jnp.sum(scores_, axis=-1, keepdims=True)
            idx = jnp.arange(S)
            position_effect = jnp.abs(idx[:, None] - idx[None, :]).astype(jnp.float32)[None, None]
            dist_scores = jnp.sqrt(jnp.clip((disttotal - distcum) * position_effect, 0.0, None))
            gamma = -jax.nn.softplus(gammas)[None]
            total_effect = jnp.clip(jnp.exp(dist_scores * gamma), 1e-05, 100000.0)
            total_effect = jax.lax.stop_gradient(total_effect)
            scores = scores * total_effect
            scores = jnp.where(allow, scores, NEG)
            attn = jax.nn.softmax(scores, axis=-1)
            out = jnp.einsum('bhqk,bhkd->bhqd', attn, v)
            concat = out.transpose(0, 2, 1, 3).reshape(B, S, D)
            query2 = concat @ Wo.T + bo
            x = _layer_norm(query + query2, ln1_w, ln1_b)
            ff = jax.nn.relu(x @ W1.T + b1) @ W2.T + b2
            x = _layer_norm(x + ff, ln2_w, ln2_b)
            return x
        key = jax.random.key(seed)
        ks = jax.random.split(key, 10)
        B, S, D, H, F = (2, 512, 256, 16, 1024)
        s = 0.02
        return {'query': jax.random.normal(ks[0], (B, S, D), jnp.float32), 'key': jax.random.normal(ks[1], (B, S, D), jnp.float32), 'values': jax.random.normal(ks[2], (B, S, D), jnp.float32), 'Wk': jax.random.normal(ks[3], (D, D), jnp.float32) * s, 'bk': jnp.zeros((D,), jnp.float32), 'Wv': jax.random.normal(ks[4], (D, D), jnp.float32) * s, 'bv': jnp.zeros((D,), jnp.float32), 'Wo': jax.random.normal(ks[5], (D, D), jnp.float32) * s, 'bo': jnp.zeros((D,), jnp.float32), 'gammas': jax.random.normal(ks[6], (H, 1, 1), jnp.float32), 'ln1_w': jnp.ones((D,), jnp.float32), 'ln1_b': jnp.zeros((D,), jnp.float32), 'W1': jax.random.normal(ks[7], (F, D), jnp.float32) * s, 'b1': jnp.zeros((F,), jnp.float32), 'W2': jax.random.normal(ks[8], (D, F), jnp.float32) * s, 'b2': jnp.zeros((D,), jnp.float32), 'ln2_w': jnp.ones((D,), jnp.float32), 'ln2_b': jnp.zeros((D,), jnp.float32), 'mask': 1}
    _L0_xattn_all = _L0_xattn_setup()
    _L0_xattn_in = {k: v for k, v in _L0_xattn_all.items() if k in ('Wk', 'bk', 'Wv', 'bv', 'Wo', 'bo', 'gammas', 'ln1_w', 'ln1_b', 'W1', 'b1', 'W2', 'b2', 'ln2_w', 'ln2_b')}
    del _L0_xattn_all

    def _L1_xattn_setup():
        import jax, jax.numpy as jnp
        import numpy as np
        D = 256
        D_STATE = 128
        N_HEADS = 8
        D_INNER = 2 * D
        HEADDIM = 64
        H_M = D_INNER // HEADDIM
        D_CONV = 4
        CONV_DIM = D_INNER + 2 * D_STATE
        D_IN_PROJ = 2 * D_INNER + 2 * D_STATE + H_M
        B = 1
        LQ = 256
        LK = 512
        EPS = 1e-05

        def _rms(x, w):
            return x * jax.lax.rsqrt(jnp.mean(x * x, axis=-1, keepdims=True) + EPS) * w

        def _ln(x, w, b):
            mu = jnp.mean(x, axis=-1, keepdims=True)
            v = jnp.mean((x - mu) ** 2, axis=-1, keepdims=True)
            return (x - mu) * jax.lax.rsqrt(v + EPS) * w + b

        def _mamba2_block(x, norm_w, in_proj_w, conv_w, conv_b, dt_bias, A_log, D_skip, gnorm_w, out_proj_w):
            b, L, _ = x.shape
            resid = x
            zxbcdt = _rms(x, norm_w) @ in_proj_w
            z = zxbcdt[..., :D_INNER]
            xBC = zxbcdt[..., D_INNER:D_INNER + CONV_DIM]
            dt = jax.nn.softplus(zxbcdt[..., -H_M:] + dt_bias)
            padded = jnp.pad(xBC, ((0, 0), (D_CONV - 1, 0), (0, 0)))
            conv = conv_b + sum((padded[:, k:k + L, :] * conv_w[:, k] for k in range(D_CONV)))
            xBC = jax.nn.silu(conv)
            xh = xBC[..., :D_INNER].reshape(b, L, H_M, HEADDIM)
            Bm = xBC[..., D_INNER:D_INNER + D_STATE]
            Cm = xBC[..., D_INNER + D_STATE:]
            A = -jnp.exp(A_log)
            decay = jnp.exp(dt * A)
            dbx = dt[..., None] * xh

            def step(h, inp):
                dec, u, bt, ct = inp
                h = h * dec[:, :, None, None] + u[..., None] * bt[:, None, None, :]
                y = jnp.einsum('bhpn,bn->bhp', h, ct)
                return (h, y)
            h0 = jnp.zeros((b, H_M, HEADDIM, D_STATE), x.dtype)
            xs = (decay.transpose(1, 0, 2), dbx.transpose(1, 0, 2, 3), Bm.transpose(1, 0, 2), Cm.transpose(1, 0, 2))
            _, ys = jax.lax.scan(step, h0, xs)
            y = ys.transpose(1, 0, 2, 3) + D_skip[None, None, :, None] * xh
            u = _rms(y.reshape(b, L, D_INNER) * jax.nn.silu(z), gnorm_w)
            return resid + u @ out_proj_w

        def _cross_attention(x, enc, pad_mask, ln_w, ln_b, Wq, Wk, Wv, Wo):
            b, Lq, _ = x.shape
            Lk = enc.shape[1]
            dh = D // N_HEADS
            resid = x
            xn = _ln(x, ln_w, ln_b)
            q = (xn @ Wq).reshape(b, Lq, N_HEADS, dh)
            k = (enc @ Wk).reshape(b, Lk, N_HEADS, dh)
            v = (enc @ Wv).reshape(b, Lk, N_HEADS, dh)
            scores = jnp.einsum('bqhd,bkhd->bhqk', q, k) * np.float32(1.0 / np.sqrt(dh))
            scores = jnp.where(pad_mask[:, None, None, :], jnp.float32(-1000000000.0), scores)
            p = jax.nn.softmax(scores, axis=-1)
            ctx = jnp.einsum('bhqk,bkhd->bqhd', p, v).reshape(b, Lq, D)
            return resid + ctx @ Wo
        key = jax.random.key(seed)
        ks = jax.random.split(key, 10)
        s = 0.02
        return {'x': jax.random.normal(ks[0], (B, LQ, D), jnp.float32), 'encoder_out': jax.random.normal(ks[1], (B, LK, D), jnp.float32), 'encoder_padding_mask': jnp.zeros((B, LK), dtype=bool), 'm_norm_w': jnp.ones((D,), jnp.float32), 'in_proj_w': s * jax.random.normal(ks[2], (D, D_IN_PROJ), jnp.float32), 'conv_w': s * jax.random.normal(ks[3], (CONV_DIM, D_CONV), jnp.float32), 'conv_b': jnp.zeros((CONV_DIM,), jnp.float32), 'dt_bias': jnp.full((H_M,), float(np.log(np.expm1(0.01))), jnp.float32), 'A_log': jnp.log(jnp.linspace(1.0, 16.0, H_M)).astype(jnp.float32), 'D_skip': jnp.ones((H_M,), jnp.float32), 'gnorm_w': jnp.ones((D_INNER,), jnp.float32), 'out_proj_w': s * jax.random.normal(ks[4], (D_INNER, D), jnp.float32), 'ca_ln_w': jnp.ones((D,), jnp.float32), 'ca_ln_b': jnp.zeros((D,), jnp.float32), 'Wq': s * jax.random.normal(ks[5], (D, D), jnp.float32), 'Wk': s * jax.random.normal(ks[6], (D, D), jnp.float32), 'Wv': s * jax.random.normal(ks[7], (D, D), jnp.float32), 'Wo': s * jax.random.normal(ks[8], (D, D), jnp.float32)}
    _L1_xattn_all = _L1_xattn_setup()
    _L1_xattn_in = {k: v for k, v in _L1_xattn_all.items() if k in ('m_norm_w', 'in_proj_w', 'conv_w', 'conv_b', 'dt_bias', 'A_log', 'D_skip', 'gnorm_w', 'out_proj_w', 'ca_ln_w', 'ca_ln_b', 'Wq', 'Wk', 'Wv', 'Wo')}
    del _L1_xattn_all
    return {'x': x, 'ctx_1024': ctx_1024, 'mask_1xS2_bf0': mask_1xS2_bf0, 'L0_xattn_Wk': _L0_xattn_in['Wk'], 'L0_xattn_bk': _L0_xattn_in['bk'], 'L0_xattn_Wv': _L0_xattn_in['Wv'], 'L0_xattn_bv': _L0_xattn_in['bv'], 'L0_xattn_Wo': _L0_xattn_in['Wo'], 'L0_xattn_bo': _L0_xattn_in['bo'], 'L0_xattn_gammas': _L0_xattn_in['gammas'], 'L0_xattn_ln1_w': _L0_xattn_in['ln1_w'], 'L0_xattn_ln1_b': _L0_xattn_in['ln1_b'], 'L0_xattn_W1': _L0_xattn_in['W1'], 'L0_xattn_b1': _L0_xattn_in['b1'], 'L0_xattn_W2': _L0_xattn_in['W2'], 'L0_xattn_b2': _L0_xattn_in['b2'], 'L0_xattn_ln2_w': _L0_xattn_in['ln2_w'], 'L0_xattn_ln2_b': _L0_xattn_in['ln2_b'], 'L1_xattn_m_norm_w': _L1_xattn_in['m_norm_w'], 'L1_xattn_in_proj_w': _L1_xattn_in['in_proj_w'], 'L1_xattn_conv_w': _L1_xattn_in['conv_w'], 'L1_xattn_conv_b': _L1_xattn_in['conv_b'], 'L1_xattn_dt_bias': _L1_xattn_in['dt_bias'], 'L1_xattn_A_log': _L1_xattn_in['A_log'], 'L1_xattn_D_skip': _L1_xattn_in['D_skip'], 'L1_xattn_gnorm_w': _L1_xattn_in['gnorm_w'], 'L1_xattn_out_proj_w': _L1_xattn_in['out_proj_w'], 'L1_xattn_ca_ln_w': _L1_xattn_in['ca_ln_w'], 'L1_xattn_ca_ln_b': _L1_xattn_in['ca_ln_b'], 'L1_xattn_Wq': _L1_xattn_in['Wq'], 'L1_xattn_Wk': _L1_xattn_in['Wk'], 'L1_xattn_Wv': _L1_xattn_in['Wv'], 'L1_xattn_Wo': _L1_xattn_in['Wo']}

def reference(x, ctx_1024, mask_1xS2_bf0, L0_xattn_Wk, L0_xattn_bk, L0_xattn_Wv, L0_xattn_bv, L0_xattn_Wo, L0_xattn_bo, L0_xattn_gammas, L0_xattn_ln1_w, L0_xattn_ln1_b, L0_xattn_W1, L0_xattn_b1, L0_xattn_W2, L0_xattn_b2, L0_xattn_ln2_w, L0_xattn_ln2_b, L1_xattn_m_norm_w, L1_xattn_in_proj_w, L1_xattn_conv_w, L1_xattn_conv_b, L1_xattn_dt_bias, L1_xattn_A_log, L1_xattn_D_skip, L1_xattn_gnorm_w, L1_xattn_out_proj_w, L1_xattn_ca_ln_w, L1_xattn_ca_ln_b, L1_xattn_Wq, L1_xattn_Wk, L1_xattn_Wv, L1_xattn_Wo):
    import jax
    import jax.numpy as jnp

    def _L0_xattn_ref(query, key, values, Wk, bk, Wv, bv, Wo, bo, gammas, ln1_w, ln1_b, W1, b1, W2, b2, ln2_w, ln2_b, mask):
        import jax, jax.numpy as jnp
        import numpy as np
        NEG = -1e+32
        EPS_LN = 1e-05

        def _layer_norm(x, w, b):
            mu = jnp.mean(x, axis=-1, keepdims=True)
            var = jnp.mean((x - mu) ** 2, axis=-1, keepdims=True)
            return (x - mu) / jnp.sqrt(var + EPS_LN) * w + b

        def _forward(query, key, values, Wk, bk, Wv, bv, Wo, bo, gammas, ln1_w, ln1_b, W1, b1, W2, b2, ln2_w, ln2_b, mask):
            B, S, D = query.shape
            H = gammas.shape[0]
            dk = D // H

            def proj(x, W, b):
                return (x @ W.T + b).reshape(B, S, H, dk).transpose(0, 2, 1, 3)
            q = proj(query, Wk, bk)
            k = proj(key, Wk, bk)
            v = proj(values, Wv, bv)
            scores = jnp.einsum('bhqd,bhkd->bhqk', q, k) / np.sqrt(dk).astype(np.float32)
            allow = jnp.tril(jnp.ones((S, S), bool), k=mask - 1)[None, None]
            scores_ = jax.nn.softmax(jnp.where(allow, scores, NEG), axis=-1)
            scores_ = scores_ * allow.astype(scores_.dtype)
            distcum = jnp.cumsum(scores_, axis=-1)
            disttotal = jnp.sum(scores_, axis=-1, keepdims=True)
            idx = jnp.arange(S)
            position_effect = jnp.abs(idx[:, None] - idx[None, :]).astype(jnp.float32)[None, None]
            dist_scores = jnp.sqrt(jnp.clip((disttotal - distcum) * position_effect, 0.0, None))
            gamma = -jax.nn.softplus(gammas)[None]
            total_effect = jnp.clip(jnp.exp(dist_scores * gamma), 1e-05, 100000.0)
            total_effect = jax.lax.stop_gradient(total_effect)
            scores = scores * total_effect
            scores = jnp.where(allow, scores, NEG)
            attn = jax.nn.softmax(scores, axis=-1)
            out = jnp.einsum('bhqk,bhkd->bhqd', attn, v)
            concat = out.transpose(0, 2, 1, 3).reshape(B, S, D)
            query2 = concat @ Wo.T + bo
            x = _layer_norm(query + query2, ln1_w, ln1_b)
            ff = jax.nn.relu(x @ W1.T + b1) @ W2.T + b2
            x = _layer_norm(x + ff, ln2_w, ln2_b)
            return x
        return _forward(query, key, values, Wk, bk, Wv, bv, Wo, bo, gammas, ln1_w, ln1_b, W1, b1, W2, b2, ln2_w, ln2_b, mask)

    def _L1_xattn_ref(x, encoder_out, encoder_padding_mask, m_norm_w, in_proj_w, conv_w, conv_b, dt_bias, A_log, D_skip, gnorm_w, out_proj_w, ca_ln_w, ca_ln_b, Wq, Wk, Wv, Wo):
        import jax, jax.numpy as jnp
        import numpy as np
        D = 256
        D_STATE = 128
        N_HEADS = 8
        D_INNER = 2 * D
        HEADDIM = 64
        H_M = D_INNER // HEADDIM
        D_CONV = 4
        CONV_DIM = D_INNER + 2 * D_STATE
        D_IN_PROJ = 2 * D_INNER + 2 * D_STATE + H_M
        B = 1
        LQ = 256
        LK = 512
        EPS = 1e-05

        def _rms(x, w):
            return x * jax.lax.rsqrt(jnp.mean(x * x, axis=-1, keepdims=True) + EPS) * w

        def _ln(x, w, b):
            mu = jnp.mean(x, axis=-1, keepdims=True)
            v = jnp.mean((x - mu) ** 2, axis=-1, keepdims=True)
            return (x - mu) * jax.lax.rsqrt(v + EPS) * w + b

        def _mamba2_block(x, norm_w, in_proj_w, conv_w, conv_b, dt_bias, A_log, D_skip, gnorm_w, out_proj_w):
            b, L, _ = x.shape
            resid = x
            zxbcdt = _rms(x, norm_w) @ in_proj_w
            z = zxbcdt[..., :D_INNER]
            xBC = zxbcdt[..., D_INNER:D_INNER + CONV_DIM]
            dt = jax.nn.softplus(zxbcdt[..., -H_M:] + dt_bias)
            padded = jnp.pad(xBC, ((0, 0), (D_CONV - 1, 0), (0, 0)))
            conv = conv_b + sum((padded[:, k:k + L, :] * conv_w[:, k] for k in range(D_CONV)))
            xBC = jax.nn.silu(conv)
            xh = xBC[..., :D_INNER].reshape(b, L, H_M, HEADDIM)
            Bm = xBC[..., D_INNER:D_INNER + D_STATE]
            Cm = xBC[..., D_INNER + D_STATE:]
            A = -jnp.exp(A_log)
            decay = jnp.exp(dt * A)
            dbx = dt[..., None] * xh

            def step(h, inp):
                dec, u, bt, ct = inp
                h = h * dec[:, :, None, None] + u[..., None] * bt[:, None, None, :]
                y = jnp.einsum('bhpn,bn->bhp', h, ct)
                return (h, y)
            h0 = jnp.zeros((b, H_M, HEADDIM, D_STATE), x.dtype)
            xs = (decay.transpose(1, 0, 2), dbx.transpose(1, 0, 2, 3), Bm.transpose(1, 0, 2), Cm.transpose(1, 0, 2))
            _, ys = jax.lax.scan(step, h0, xs)
            y = ys.transpose(1, 0, 2, 3) + D_skip[None, None, :, None] * xh
            u = _rms(y.reshape(b, L, D_INNER) * jax.nn.silu(z), gnorm_w)
            return resid + u @ out_proj_w

        def _cross_attention(x, enc, pad_mask, ln_w, ln_b, Wq, Wk, Wv, Wo):
            b, Lq, _ = x.shape
            Lk = enc.shape[1]
            dh = D // N_HEADS
            resid = x
            xn = _ln(x, ln_w, ln_b)
            q = (xn @ Wq).reshape(b, Lq, N_HEADS, dh)
            k = (enc @ Wk).reshape(b, Lk, N_HEADS, dh)
            v = (enc @ Wv).reshape(b, Lk, N_HEADS, dh)
            scores = jnp.einsum('bqhd,bkhd->bhqk', q, k) * np.float32(1.0 / np.sqrt(dh))
            scores = jnp.where(pad_mask[:, None, None, :], jnp.float32(-1000000000.0), scores)
            p = jax.nn.softmax(scores, axis=-1)
            ctx = jnp.einsum('bhqk,bkhd->bqhd', p, v).reshape(b, Lq, D)
            return resid + ctx @ Wo
        h = _mamba2_block(x, m_norm_w, in_proj_w, conv_w, conv_b, dt_bias, A_log, D_skip, gnorm_w, out_proj_w)
        return _cross_attention(h, encoder_out, encoder_padding_mask, ca_ln_w, ca_ln_b, Wq, Wk, Wv, Wo)
    x = _L0_xattn_ref(x, ctx_1024, ctx_1024, L0_xattn_Wk, L0_xattn_bk, L0_xattn_Wv, L0_xattn_bv, L0_xattn_Wo, L0_xattn_bo, L0_xattn_gammas, L0_xattn_ln1_w, L0_xattn_ln1_b, L0_xattn_W1, L0_xattn_b1, L0_xattn_W2, L0_xattn_b2, L0_xattn_ln2_w, L0_xattn_ln2_b, 1)
    x = _L1_xattn_ref(x, ctx_1024, mask_1xS2_bf0, L1_xattn_m_norm_w, L1_xattn_in_proj_w, L1_xattn_conv_w, L1_xattn_conv_b, L1_xattn_dt_bias, L1_xattn_A_log, L1_xattn_D_skip, L1_xattn_gnorm_w, L1_xattn_out_proj_w, L1_xattn_ca_ln_w, L1_xattn_ca_ln_b, L1_xattn_Wq, L1_xattn_Wk, L1_xattn_Wv, L1_xattn_Wo)
    return x

_drawn_inputs = setup_inputs


def setup_inputs(seed=0):
    import zlib

    import numpy as np

    out = dict(_drawn_inputs(seed))
    spreads = {'L0_xattn_bk': (0.0, 0.8),
     'L0_xattn_bv': (0.0, 0.1),
     'L0_xattn_bo': (0.0, 0.1),
     'L0_xattn_ln1_w': (1.0, 0.2),
     'L0_xattn_ln1_b': (0.0, 0.1),
     'L0_xattn_b1': (0.0, 0.1),
     'L0_xattn_b2': (0.0, 0.1),
     'L0_xattn_ln2_w': (1.0, 0.2),
     'L0_xattn_ln2_b': (0.0, 0.1),
     'L1_xattn_m_norm_w': (1.0, 0.2),
     'L1_xattn_conv_b': (0.0, 0.1),
     'L1_xattn_dt_bias': (-4.600165843963623, 0.6),
     'L1_xattn_D_skip': (1.0, 0.2),
     'L1_xattn_gnorm_w': (1.0, 0.2),
     'L1_xattn_ca_ln_w': (1.0, 0.6),
     'L1_xattn_ca_ln_b': (0.0, 0.8)}
    factors = {'L0_xattn_Wk': 8.0,
     'L0_xattn_gammas': 8.0,
     'L1_xattn_A_log': 8.0,
     'L1_xattn_Wq': 8.0,
     'L1_xattn_Wk': 8.0}
    for name, (base, spread) in spreads.items():
        noise = np.random.default_rng([zlib.crc32(name.encode()), seed]).standard_normal(out[name].shape)
        drawn = base * np.exp(spread * noise) if base else spread * noise
        out[name] = jnp.asarray(drawn.astype(out[name].dtype))
    for name, factor in factors.items():
        out[name] = (out[name] * factor).astype(out[name].dtype)
    return out
```

```python
from contextlib import ExitStack

import concourse.bass as bass
from concourse import mybir

F32 = mybir.dt.float32
F32R = mybir.dt.float32r
BF16 = mybir.dt.bfloat16
U8 = mybir.dt.uint8
ALU = mybir.AluOpType
ACT = mybir.ActivationFunctionType
AX = mybir.AxisListType.X

P = 128
PAIR = 2
T2 = PAIR * P
D = 256
KC = D // P
H0, DH0 = 16, 16
F = 1024
FM = F // P
DI = 512
HM, HD = 8, 64
CM = 6
TAPS = 4
H1, DH1 = 8, 32
EPS = 1e-5
TINY = 1e-19
SIG_MAX = 1e19
POS = 22
UA = 8
UC = 4
CHUNKS = [(4, 6), (0, 2), (2, 4)]


class Signal:

    def __init__(self, sem, per_pair):
        self.sem, self.per_pair = sem, per_pair

    def at(self, p, k):
        value = p * self.per_pair + k
        return max(value, 0) if isinstance(value, int) else value


def build(nc, a, out):
    NSEQ = out.shape[1]
    NP = NSEQ // PAIR
    ctx = ExitStack()
    with ctx:
        def sb(name, shape, dt=F32):
            return ctx.enter_context(nc.sbuf_tensor(name, shape, dt))

        def bank(name):
            return ctx.enter_context(nc.psum_tensor(name, [P, 512], F32))

        def sig(name, per_pair):
            return Signal(ctx.enter_context(nc.semaphore(name)), per_pair)

        ident = sb("ident", [P, P])
        identb = sb("identb", [P, P], BF16)
        minus = sb("minus", [P, P], F32R)
        later = sb("later", [P, P])
        tri = sb("tri", [P, P])
        causal = sb("causal", [P, 4 * P], BF16)
        padmask = sb("padmask", [P, 4 * P], BF16)
        eye4 = sb("eye4", [P, 4 * P])
        dist = sb("dist", [P, P])
        distg = sb("distg", [P, 4, 2, 2, P])
        half16 = sb("half16", [P, 2])
        half32 = sb("half32", [P, 2])
        wk0 = sb("wk0", [P, KC, D])
        wv0 = sb("wv0", [P, KC, D])
        wo0 = sb("wo0", [P, KC, D])
        w1 = sb("w1", [P, KC, F])
        w2 = sb("w2", [P, FM, D])
        win = sb("win", [P, KC, 2 * DI + 2 * P + HM])
        wout = sb("wout", [P, DI // P, D])
        wq1 = sb("wq1", [P, KC, D])
        wk1 = sb("wk1", [P, KC, D])
        wv1 = sb("wv1", [P, KC, D])
        wo1 = sb("wo1", [P, KC, D])
        bk0 = sb("bk0", [P, KC])
        qb0 = sb("qb0", [P, KC, 2])
        qb1 = sb("qb1", [P, KC, 2])
        b1 = sb("b1", [P, FM])
        ln1w_c = sb("ln1w_c", [P, KC])
        ln1b_c = sb("ln1b_c", [P, KC])
        nw_c = sb("nw_c", [P, KC])
        gw_c = sb("gw_c", [P, DI // P])
        lw_c = sb("lw_c", [P, KC])
        lb_c = sb("lb_c", [P, KC])
        convw = sb("convw", [P, CM, TAPS])
        convb = sb("convb", [P, CM])
        dtb = sb("dtb", [HM, 1])
        nega = sb("nega", [HM, 1])
        bv_r = sb("bv_r", [P, D])
        bo_r = sb("bo_r", [P, D])
        b2_r = sb("b2_r", [P, D])
        ln1w_r = sb("ln1w_r", [P, D])
        ln1b_r = sb("ln1b_r", [P, D])
        ln2w_r = sb("ln2w_r", [P, D])
        ln2b_r = sb("ln2b_r", [P, D])
        dskip_r = sb("dskip_r", [P, HM])
        gam = sb("gam", [P, H0])
        gabs = sb("gabs", [P, H0])
        mask8 = sb("mask8", [P, P], U8)
        eps_c = sb("eps_c", [P, 1])
        tiny_c = sb("tiny_c", [P, 1])

        xT = sb("xT", [P, KC, T2])
        cT = sb("cT", [P, KC, T2])
        q0 = sb("q0", [P, KC, 2, T2])
        k0 = sb("k0", [P, KC, T2])
        v0 = sb("v0", [P, PAIR, H0, DH0 + 1])
        sc0 = sb("sc0", [P, 4, 4 * P])
        m1 = sb("m1", [P, 2, 4])
        m2 = sb("m2", [P, 2, 4])
        dg1 = sb("dg1", [P, 2, 4 * P], F32R)
        dg2 = sb("dg2", [P, 2, 4 * P], F32R)
        e0 = sb("e0", [P, 2, 4 * P])
        rz = sb("rz", [P, 2, 4])
        dec0 = sb("dec0", [P, 2, 4 * P])
        e1 = sb("e1", [P, 2, 4 * P])
        rz2 = sb("rz2", [P, H0])
        att = sb("att", [P, PAIR, D])
        xin = sb("xin", [P, PAIR, D])
        xb = sb("xb", [P, PAIR, D])
        attT = sb("attT", [P, KC, T2])
        s1 = sb("s1", [P, PAIR, D])
        st1 = sb("st1", [P, PAIR, 6])
        mv1 = sb("mv1", [P, PAIR, 2])
        rs1 = sb("rs1", [P, PAIR])
        x1T = sb("x1T", [P, KC, T2])
        x1b = sb("x1b", [P, PAIR, D])
        hT = sb("hT", [P, FM, T2])
        st2 = sb("st2", [P, PAIR, 6])
        mv2 = sb("mv2", [P, PAIR, 2])
        rs2 = sb("rs2", [P, PAIR])
        x2 = sb("x2", [P, PAIR, D])
        ms = sb("ms", [P, PAIR])
        xnT = sb("xnT", [P, KC, T2])
        resid = sb("resid", [P, PAIR, D])
        cin = sb("cin", [P, CM, PAIR, TAPS - 1 + P])
        esig = cin[:, :, :, TAPS - 1:].rearrange("q m b t -> q (m b) t")
        acc = sb("acc", [P, CM, T2])
        acc_v = acc[:].rearrange("q m (b t) -> q (m b) t", b=PAIR)
        xc = acc
        dtv = sb("dtv", [HM, T2])
        dtp = sb("dtp", [HM, T2])
        dta = sb("dta", [HM, T2])
        sp = sb("sp", [HM, T2])
        decay = sb("decay", [HM, PAIR, P])
        zc = sb("zc", [P, PAIR, DI])
        ez = sb("ez", [P, PAIR, DI])
        zs = ez
        g = sb("g", [P, PAIR, HM * P])
        cbdt = sb("cbdt", [P, 2 * P + PAIR * HM])
        dtx = sb("dtx", [P, PAIR, DI])
        y = sb("y", [P, PAIR, DI])
        sqy = sb("sqy", [P, DI])
        ssq = sb("ssq", [P, PAIR])
        yT = dtx
        h = sb("h", [P, PAIR, D])
        cTc = sb("cTc", [P, KC, T2])
        hres = sb("hres", [P, PAIR, D])
        k1 = sb("k1", [P, KC, T2])
        v1 = sb("v1", [P, PAIR, H1, DH1 + 1])
        st3 = sb("st3", [P, PAIR, 6])
        mv3 = sb("mv3", [P, PAIR, 2])
        rs3 = sb("rs3", [P, PAIR])
        xh3T = sb("xh3T", [P, KC, T2])
        q1 = sb("q1", [P, KC, 2, T2])
        m3 = sb("m3", [P, 2, 4])
        sc3 = sb("sc3", [P, 1, 4 * P])
        dg3 = sb("dg3", [P, 1, 4 * P], F32R)
        e3 = sb("e3", [P, 1, 4 * P])
        rz3 = sb("rz3", [P, 4])
        co = sb("co", [P, PAIR, D])
        coT = sb("coT", [P, KC, T2])
        res = co

        scores, turned, sums, attn_out = bank("scores"), bank("turned"), bank("sums"), bank("attn_out")
        ffn = bank("ffn")
        mamba = [bank("mamba0"), bank("mamba1")]
        cross = bank("cross")

        loaded = sig("loaded", 0)
        set_up = sig("set_up", 0)
        a_loaded = sig("a_loaded", 32)
        q_proj, k_proj, v_proj = sig("q_proj", 1), sig("k_proj", 1), sig("v_proj", 1)
        q_ready, k_ready, v_ready = sig("q_ready", 1), sig("k_ready", 1), sig("v_ready", 1)
        scored, maxed, copied = sig("scored", UA), sig("maxed", UA), sig("copied", UA)
        diag1, turned1, exp1 = sig("diag1", UA), sig("turned1", UA), sig("exp1", UA)
        summed, recip1, distanced = sig("summed", UA), sig("recip1", UA), sig("distanced", UA)
        normed = sig("normed", UA)
        log_d, root_d, effect = sig("log_d", UA), sig("root_d", UA), sig("effect", UA)
        decayed, maxed2, diag2 = sig("decayed", UA), sig("maxed2", UA), sig("diag2", UA)
        turned2, exp2, weighed = sig("turned2", UA), sig("exp2", UA), sig("weighed", UA)
        recip2, att_ready = sig("recip2", PAIR), sig("att_ready", PAIR)

        x_loaded, xb_ready = sig("x_loaded", 16), sig("xb_ready", 1)
        att_turned, attT_ready, wo_done = sig("att_turned", 1), sig("attT_ready", 1), sig("wo_done", 1)
        s1_done, st1_done, mv1_done = sig("s1_done", 1), sig("st1_done", 1), sig("mv1_done", 1)
        lg1, rs1_done, xh1_ready = sig("lg1", 1), sig("rs1_done", 1), sig("xh1_ready", 1)
        x1m_done, x1b_ready = sig("x1m_done", 1), sig("x1b_ready", 1)
        x1_turned, x1T_ready = sig("x1_turned", 1), sig("x1T_ready", 1)
        up_done, relu_a, relu_v = sig("up_done", 4), sig("relu_a", 2), sig("relu_v", 2)
        down_done = sig("down_done", 1)
        s2_done, st2_done, mv2_done = sig("s2_done", 1), sig("st2_done", 1), sig("mv2_done", 1)
        lg2, rs2_done, xh2_ready = sig("lg2", 1), sig("rs2_done", 1), sig("xh2_ready", 1)
        x2m_done, x2_ready = sig("x2m_done", 1), sig("x2_ready", 1)
        sq_done, lg_r, rsr_done = sig("sq_done", PAIR), sig("lg_r", 1), sig("rsr_done", 1)
        xn_ready, xn_turned, xnT_ready = sig("xn_ready", 1), sig("xn_turned", 1), sig("xnT_ready", 1)

        resid_ready = sig("resid_ready", 1)
        xbc_done, conv_in = sig("xbc_done", 3), sig("conv_in", 3)
        tap_done = sig("tap_done", 18)
        esig_done, eclip, lnsig, sigm = sig("esig_done", 3), sig("eclip", 3), sig("lnsig", 3), sig("sigm", 3)
        xc_ready = sig("xc_ready", 3)
        dt_raw = sig("dt_raw", 1)
        dt_done, dt_pos, dt_abs = sig("dt_done", 1), sig("dt_pos", 1), sig("dt_abs", 1)
        dt_exp, dt_log, sp_ready, decay_ready = sig("dt_exp", 1), sig("dt_log", 1), sig("sp_ready", 1), sig("decay_ready", 1)
        z_done, z_exp, z_clip, z_log, z_sig, zs_ready = (sig(n, PAIR) for n in (
            "z_done", "z_exp", "z_clip", "z_log", "z_sig", "zs_ready"))
        spread, scanned = sig("spread", 4), sig("scanned", 4)
        cb_done, cb_ready = sig("cb_done", 1), sig("cb_ready", 1)
        mixed, x_turned, xtok = sig("mixed", PAIR), sig("x_turned", PAIR), sig("xtok", PAIR)
        y_done, y_skip, y_gated, ysq = sig("y_done", PAIR), sig("y_skip", PAIR), sig("y_gated", PAIR), sig("ysq", PAIR)
        lg_g, rsg_done = sig("lg_g", 1), sig("rsg_done", 1)
        y_turned, yT_ready = sig("y_turned", PAIR), sig("yT_ready", PAIR)
        mout_done, h_ready = sig("mout_done", 1), sig("h_ready", 1)

        c_loaded = sig("c_loaded", 16)
        k1_proj, k1_ready, v1_proj, v1_ready = sig("k1_proj", 1), sig("k1_ready", 1), sig("v1_proj", 1), sig("v1_ready", 1)
        hres_ready, st3_done, mv3_done = sig("hres_ready", 1), sig("st3_done", 1), sig("mv3_done", 1)
        lg3, rs3_done, xh3_ready = sig("lg3", 1), sig("rs3_done", 1), sig("xh3_ready", 1)
        xh3_turned, xh3T_ready = sig("xh3_turned", 1), sig("xh3T_ready", 1)
        q1_proj, q1_ready = sig("q1_proj", 1), sig("q1_ready", 1)
        scored3, maxed3, copied3 = sig("scored3", UC), sig("maxed3", UC), sig("copied3", UC)
        diag3, turned3, exp3 = sig("diag3", UC), sig("turned3", UC), sig("exp3", UC)
        weighed3, recip3, co_ready = sig("weighed3", UC), sig("recip3", UC), sig("co_ready", UC)
        co_turned, coT_ready, out_proj = sig("co_turned", 1), sig("coT_ready", 1), sig("out_proj", 1)
        out_ready, stored = sig("out_ready", 1), sig("stored", 16)

        block = ctx.enter_context(nc.Block())

        def run(engine, body):
            def active(i):
                return [0 <= i - lag < NP for lag in range(4)]
            for i in range(4):
                body(i, active(i))
            with engine.Fori(4, NP) as i:
                body(i, [True] * 4)
            for i in range(NP, NP + 3):
                body(i, active(i))

        def rows(ap, n):
            return ap.rearrange("(o n) -> o n", o=1).broadcast_to([P, n])

        LOADS = [
            (ident, a["ident"]), (tri, a["tri"]), (later, a["later"]),
            (eye4, a["eye4"]), (dist, a["dist"]), (half16, a["half16"]), (half32, a["half32"]),
            (wk0, a["wk0"]), (wv0, a["wv0"]), (bk0, a["bk0"]), (bv_r, rows(a["bv0"], D)), (gam, rows(a["gammas"], H0)),
            (mask8, rows(a["mask"], P)),
            (lw_c, a["ca_ln_w"]), (lb_c, a["ca_ln_b"]), (wq1, a["wq1"]),
            (win, a["win"]), (nw_c, a["m_norm_w"]), (wout, a["wout"]), (gw_c, a["gnorm_w"]),
            (wo0, a["wo0"]), (w1, a["w1"]), (w2, a["w2"]), (wk1, a["wk1"]), (wv1, a["wv1"]), (wo1, a["wo1"]),
            (b1, a["b1"]), (ln1w_c, a["ln1_w"]), (ln1b_c, a["ln1_b"]), (convw, a["conv_w"]), (convb, a["conv_b"]),
            (dtb, a["dt_bias"]), (nega, a["A_log"]),
            (bo_r, rows(a["bo0"], D)), (b2_r, rows(a["b2"], D)),
            (ln1w_r, rows(a["ln1_w_row"], D)), (ln1b_r, rows(a["ln1_b_row"], D)),
            (ln2w_r, rows(a["ln2_w_row"], D)), (ln2b_r, rows(a["ln2_b_row"], D)),
            (dskip_r, rows(a["D_skip"], HM)),
        ]
        ALL_LOADED = 16 * len(LOADS)

        @block.sync
        def _(sp_):
            eng = sp_
            xT_d = a["xT"].rearrange("(c q) t -> q c t", q=P)
            cT_d = a["cT"].rearrange("(c q) t -> q c t", q=P)
            x_d = a["x"]

            def load_a(p):
                eng.dma_start(xT[:], xT_d[:, :, bass.ts(p, T2)]).then_inc(a_loaded.sem, 16)
                eng.dma_start(cT[:], cT_d[:, :, bass.ts(p, T2)]).then_inc(a_loaded.sem, 16)

            def body(i, act_a, act_x, act_c, act_out):
                if act_a:
                    eng.wait_ge(v_proj.sem, v_proj.at(i, 1))
                    load_a(i + 1)
                if act_x:
                    eng.wait_ge(xb_ready.sem, xb_ready.at(i - 1, 1))
                    eng.dma_start(xin[:], x_d[:, bass.ts(i, PAIR), :]).then_inc(x_loaded.sem, 16)
                if act_c:
                    eng.wait_ge(v1_proj.sem, v1_proj.at(i - 3, 1))
                    eng.dma_start(cTc[:], cT_d[:, :, bass.ts(i - 2, T2)]).then_inc(c_loaded.sem, 16)
                if act_out:
                    eng.wait_ge(out_ready.sem, out_ready.at(i - 3, 1))
                    eng.dma_start(out[:, bass.ts(i - 3, PAIR), :], res[:]).then_inc(stored.sem, 16)

            load_a(0)
            for dst, src in LOADS:
                eng.dma_start(dst[:], src).then_inc(loaded.sem, 16)

            def flags(i):
                return i + 1 < NP, i < NP, 0 <= i - 2 < NP, 0 <= i - 3 < NP
            for i in range(3):
                body(i, *flags(i))
            with eng.Fori(3, NP - 1) as i:
                body(i, True, True, True, True)
            for i in range(NP - 1, NP + 3):
                body(i, *flags(i))
            eng.wait_ge(stored.sem, 16 * NP)

        @block.gpsimd
        def _(pool):
            V = nc.gpsimd

            V.memset(v0[:], 1.0)
            V.memset(v1[:], 1.0)
            V.memset(cin[:], 0.0)
            V.memset(decay[:], 0.0)
            V.memset(eps_c[:], EPS)
            V.memset(tiny_c[:], TINY).then_inc(set_up.sem, 1)
            pool.wait_ge(loaded.sem, ALL_LOADED)
            pool.wait_ge(set_up.sem, SETUP_DONE)

            def diag(u_sig, dg, m, src_sig, reader_sig, p, u):
                pool.wait_ge(src_sig.sem, src_sig.at(p, u + 1))
                pool.wait_ge(reader_sig.sem, reader_sig.at(p, u - 1))
                if True:
                    V.tensor_tensor(dg[:, u % 2, :].rearrange("q (n k) -> q n k", n=4),
                                    ident[:].unsqueeze(1).broadcast_to([P, 4, P]),
                                    m[:, u % 2, :].unsqueeze(2).broadcast_to([P, 4, P]),
                                    ALU.mult).then_inc(u_sig.sem, 1)

            def attention(pos, p):
                s = pos // 2
                if pos % 2 == 0:
                    if 0 <= s - 2 < UA:
                        u = s - 2
                        pool.wait_ge(distanced.sem, distanced.at(p, u + 1))
                        d = dec0[:, u % 2, :].rearrange("q (n k) -> q n k", n=4)
                        V.tensor_tensor(d, d, rz[:, u % 2, :].unsqueeze(2).broadcast_to([P, 4, P]),
                                        ALU.mult).then_inc(normed.sem, 1)
                    if s < UA:
                        diag(diag1, dg1, m1, maxed, turned1, p, s)
                    if 0 <= s - 2 < UA:
                        diag(diag2, dg2, m2, maxed2, turned2, p, s - 2)

            def ffn_stage(pos, p):
                if pos == 0:
                    pool.wait_ge(x_loaded.sem, x_loaded.at(p, 16))
                    pool.wait_ge(s1_done.sem, s1_done.at(p - 1, 1))
                    V.tensor_tensor(xb[:], xin[:], bo_r[:].unsqueeze(1).broadcast_to([P, PAIR, D]),
                                    ALU.add).then_inc(xb_ready.sem, 1)
                if pos == 5:
                    pool.wait_ge(xh1_ready.sem, xh1_ready.at(p, 1))
                    V.tensor_tensor(x1b[:], s1[:], ln1w_r[:].unsqueeze(1).broadcast_to([P, PAIR, D]),
                                    ALU.mult).then_inc(x1m_done.sem, 1)
                    pool.wait_ge(x1m_done.sem, x1m_done.at(p, 1))
                    V.tensor_tensor(x1b[:], x1b[:], ln1b_r[:].unsqueeze(1).broadcast_to([P, PAIR, D]),
                                    ALU.add).then_inc(x1b_ready.sem, 1)
                if pos == 15:
                    pool.wait_ge(xh2_ready.sem, xh2_ready.at(p, 1))
                    pool.wait_ge(resid_ready.sem, resid_ready.at(p - 1, 1))
                    V.tensor_tensor(x2[:], s1[:], ln2w_r[:].unsqueeze(1).broadcast_to([P, PAIR, D]),
                                    ALU.mult).then_inc(x2m_done.sem, 1)
                    pool.wait_ge(x2m_done.sem, x2m_done.at(p, 1))
                    V.tensor_tensor(x2[:], x2[:], ln2b_r[:].unsqueeze(1).broadcast_to([P, PAIR, D]),
                                    ALU.add).then_inc(x2_ready.sem, 1)

            def mamba_stage(pos, p):
                if pos in (7, 8):
                    b = pos - 7
                    pool.wait_ge(z_sig.sem, z_sig.at(p, b + 1))
                    V.tensor_tensor(zs[:, b, :], zc[:, b, :], ez[:, b, :], ALU.mult).then_inc(zs_ready.sem, 1)

            def cross_stage(pos, p):
                v, r = divmod(pos - 5, 3)
                if pos >= 5 and r == 0 and v < UC:
                    pool.wait_ge(maxed3.sem, maxed3.at(p, v + 1))
                    pool.wait_ge(turned3.sem, turned3.at(p, v))
                    V.tensor_tensor(dg3[:, 0, :].rearrange("q (n k) -> q n k", n=4),
                                    ident[:].unsqueeze(1).broadcast_to([P, 4, P]),
                                    m3[:, v % 2, :].unsqueeze(2).broadcast_to([P, 4, P]),
                                    ALU.mult).then_inc(diag3.sem, 1)

            def body(i, on):
                for pos in range(POS):
                    if on[0]:
                        attention(pos, i)
                    if on[1]:
                        ffn_stage(pos, i - 1)
                    if on[2]:
                        mamba_stage(pos, i - 2)
                    if on[3]:
                        cross_stage(pos, i - 3)
            run(pool, body)

        @block.scalar
        def _(act):
            S = nc.scalar
            act.preload_act_table_set("natural_log_exp_and_others")
            act.wait_ge(loaded.sem, ALL_LOADED)
            act.wait_ge(set_up.sem, 1)
            S.activation(gabs[:], gam[:], ACT.Abs).then_inc(set_up.sem, 1)
            act.wait_ge(set_up.sem, 2)
            S.activation(gabs[:], gabs[:], ACT.Exp, scale=-1.0).then_inc(set_up.sem, 1)
            act.wait_ge(set_up.sem, 3)
            S.activation(gabs[:], gabs[:], ACT.Ln, bias=1.0).then_inc(set_up.sem, 1)
            S.activation(nega[:], nega[:], ACT.Exp).then_inc(set_up.sem, 1)
            act.wait_ge(set_up.sem, SETUP_DONE)

            def rsqrt(v_in, v_out, scale, done_log, done, p):
                S.activation(v_out, v_in, ACT.Ln, bias=eps_c[:], scale=scale).then_inc(done_log.sem, 1)
                act.wait_ge(done_log.sem, done_log.at(p, 1))
                S.activation(v_out, v_out, ACT.Exp, scale=-0.5).then_inc(done.sem, 1)

            def attention(pos, p):
                s = pos // 2
                if pos == 0:
                    act.wait_ge(q_proj.sem, q_proj.at(p, 1))
                    for c in range(KC):
                        for par in range(2):
                            last = S.activation(q0[:, c, par, :], scores[:, c * T2:(c + 1) * T2], ACT.Identity,
                                                bias=qb0[:, c, par:par + 1], scale=half16[:, par:par + 1])
                    last.then_inc(q_ready.sem, 1)
                if pos % 2 == 0:
                    if 0 <= s - 3 < UA:
                        u = s - 3
                        act.wait_ge(turned2.sem, turned2.at(p, u + 1))
                        S.activation(e1[:, u % 2, :], turned[:], ACT.Exp).then_inc(exp2.sem, 1)
                    if s < UA:
                        act.wait_ge(scored.sem, scored.at(p, s + 1))
                        act.wait_ge(decayed.sem, decayed.at(p, s - 3))
                        S.activation(sc0[:, s % 4, :], scores[:], ACT.Copy).then_inc(copied.sem, 1)
                    if 0 <= s - 2 < UA:
                        u = s - 2
                        act.wait_ge(normed.sem, normed.at(p, u + 1))
                        S.activation(dec0[:, u % 2, :], dec0[:, u % 2, :], ACT.Ln, bias=tiny_c[:]).then_inc(log_d.sem, 1)
                elif 0 <= s - 1 < UA:
                    u = s - 1
                    act.wait_ge(turned1.sem, turned1.at(p, u + 1))
                    S.activation(e0[:, u % 2, :], turned[:], ACT.Exp).then_inc(exp1.sem, 1)

            def attention_root(pos, p):
                u = pos // 2 - 2
                if pos % 2 == 0 and 0 <= u < UA:
                    act.wait_ge(log_d.sem, log_d.at(p, u + 1))
                    S.activation(dec0[:, u % 2, :], dec0[:, u % 2, :], ACT.Exp, scale=0.5).then_inc(root_d.sem, 1)

            def attention_effect(pos, p):
                u = pos // 2 - 2
                if pos % 2 == 0 and 0 <= u < UA:
                    act.wait_ge(root_d.sem, root_d.at(p, u + 1))
                    S.activation(dec0[:, u % 2, :], dec0[:, u % 2, :], ACT.Exp, scale=-1.0).then_inc(effect.sem, 1)

            def ffn_stage(pos, p):
                if pos == 0:
                    act.wait_ge(att_turned.sem, att_turned.at(p, 1))
                    S.activation(attT[:].rearrange("q c t -> q (c t)"), ffn[:], ACT.Copy).then_inc(attT_ready.sem, 1)
                if pos == 2:
                    act.wait_ge(mv1_done.sem, mv1_done.at(p, 1))
                    rsqrt(mv1[:, :, 1], rs1[:], 1.0, lg1, rs1_done, p)
                if pos == 4:
                    act.wait_ge(x1_turned.sem, x1_turned.at(p, 1))
                    for c in range(KC):
                        last = S.activation(x1T[:, c, :], ffn[:, c * T2:(c + 1) * T2], ACT.Identity,
                                            bias=ln1b_c[:, c:c + 1], scale=ln1w_c[:, c:c + 1])
                    last.then_inc(x1T_ready.sem, 1)
                if pos in (5, 7):
                    n = pos - 5
                    act.wait_ge(up_done.sem, up_done.at(p, n + 1))
                    for c in range(2):
                        last = S.activation(hT[:, 2 * n + c, :], ffn[:, c * T2:(c + 1) * T2], ACT.Relu,
                                            bias=b1[:, 2 * n + c:2 * n + c + 1])
                    last.then_inc(relu_a.sem, 1)
                if pos == 13:
                    act.wait_ge(mv2_done.sem, mv2_done.at(p, 1))
                    rsqrt(mv2[:, :, 1], rs2[:], 1.0, lg2, rs2_done, p)
                if pos == 16:
                    act.wait_ge(x2_ready.sem, x2_ready.at(p, 1))
                    for b in range(PAIR):
                        if b:
                            act.wait_ge(sq_done.sem, sq_done.at(p, b))
                        S.activation(x1b[:, b, :], x2[:, b, :], ACT.Square,
                                     accum_out=ms[:, b:b + 1]).then_inc(sq_done.sem, 1)
                    act.wait_ge(sq_done.sem, sq_done.at(p, PAIR))
                    rsqrt(ms[:], ms[:], 1.0 / D, lg_r, rsr_done, p)
                if pos == 18:
                    act.wait_ge(xn_turned.sem, xn_turned.at(p, 1))
                    S.activation(xnT[:].rearrange("q c t -> q (c t)"), ffn[:], ACT.Copy).then_inc(xnT_ready.sem, 1)

            def mamba_stage(pos, p):
                if pos < 3:
                    lo, hi = CHUNKS[pos]
                    act.wait_ge(xbc_done.sem, xbc_done.at(p, pos + 1))
                    act.wait_ge(xc_ready.sem, xc_ready.at(p - 1, 3))
                    for n, m in enumerate(range(lo, hi)):
                        S.activation(acc[:, m, :], mamba[pos % 2][:, n * T2:(n + 1) * T2], ACT.Identity,
                                     bias=convb[:, m:m + 1], scale=convw[:, m, TAPS - 1:TAPS])
                    S.activation(esig[:, 2 * lo:2 * hi, :],
                                 mamba[pos % 2][:].rearrange("q (m t) -> q m t", t=P),
                                 ACT.Copy).then_inc(conv_in.sem, 1)
                if pos == 3:
                    act.wait_ge(dt_raw.sem, dt_raw.at(p, 1))
                    S.activation(dta[:], dtv[:], ACT.Abs).then_inc(dt_abs.sem, 1)
                if pos == 4:
                    act.wait_ge(dt_abs.sem, dt_abs.at(p, 1))
                    S.activation(dta[:], dta[:], ACT.Exp, scale=-1.0).then_inc(dt_exp.sem, 1)
                if 2 <= pos < 5:
                    lo, hi = CHUNKS[pos - 2]
                    act.wait_ge(tap_done.sem, tap_done.at(p, 6 * (pos - 1)))
                    S.activation(esig[:, 2 * lo:2 * hi, :], acc_v[:, 2 * lo:2 * hi, :], ACT.Exp, scale=-1.0).then_inc(esig_done.sem, 1)
                if pos == 4:
                    act.wait_ge(dt_exp.sem, dt_exp.at(p, 1))
                    S.activation(dta[:], dta[:], ACT.Ln, bias=1.0).then_inc(dt_log.sem, 1)
                if pos in (4, 5):
                    b = pos - 4
                    act.wait_ge(z_done.sem, z_done.at(p, b + 1))
                    act.wait_ge(y_gated.sem, y_gated.at(p - 1, PAIR))
                    S.activation(zc[:, b, :], mamba[pos % 2][:], ACT.Copy)
                    S.activation(ez[:, b, :], mamba[pos % 2][:], ACT.Exp, scale=-1.0).then_inc(z_exp.sem, 1)
                if 4 <= pos < 7:
                    lo, hi = CHUNKS[pos - 4]
                    act.wait_ge(eclip.sem, eclip.at(p, pos - 3))
                    S.activation(esig[:, 2 * lo:2 * hi, :], esig[:, 2 * lo:2 * hi, :], ACT.Ln, bias=1.0).then_inc(lnsig.sem, 1)
                if pos == 5:
                    act.wait_ge(sp_ready.sem, sp_ready.at(p, 1))
                    S.activation(decay[:, :, 1:P], sp[:].rearrange("q (b t) -> q b t", b=PAIR)[:, :, 1:P], ACT.Exp,
                                 scale=nega[:]).then_inc(decay_ready.sem, 1)
                if pos in (6, 7):
                    b = pos - 6
                    act.wait_ge(z_clip.sem, z_clip.at(p, b + 1))
                    S.activation(ez[:, b, :], ez[:, b, :], ACT.Ln, bias=1.0).then_inc(z_log.sem, 1)
                if 4 <= pos < 7:
                    lo, hi = CHUNKS[pos - 4]
                    act.wait_ge(lnsig.sem, lnsig.at(p, pos - 3))
                    S.activation(esig[:, 2 * lo:2 * hi, :], esig[:, 2 * lo:2 * hi, :], ACT.Exp, scale=-1.0).then_inc(sigm.sem, 1)
                if pos in (6, 7):
                    b = pos - 6
                    act.wait_ge(z_log.sem, z_log.at(p, b + 1))
                    S.activation(ez[:, b, :], ez[:, b, :], ACT.Exp, scale=-1.0).then_inc(z_sig.sem, 1)
                if pos == 8:
                    act.wait_ge(cb_done.sem, cb_done.at(p, 1))
                    S.activation(cbdt[:], mamba[0][:, 0:2 * P + PAIR * HM], ACT.Copy).then_inc(cb_ready.sem, 1)
                if pos in (15, 16):
                    b = pos - 15
                    act.wait_ge(y_gated.sem, y_gated.at(p, b + 1))
                    act.wait_ge(ysq.sem, ysq.at(p, b))
                    S.activation(sqy[:], y[:, b, :], ACT.Square, accum_out=ssq[:, b:b + 1]).then_inc(ysq.sem, 1)
                if pos in (17, 18):
                    b = pos - 17
                    act.wait_ge(y_turned.sem, y_turned.at(p, b + 1))
                    S.activation(yT[:, b, :], mamba[(b + 1) % 2][:], ACT.Copy).then_inc(yT_ready.sem, 1)
                if pos == 18:
                    act.wait_ge(ysq.sem, ysq.at(p, PAIR))
                    rsqrt(ssq[:], ssq[:], 1.0 / DI, lg_g, rsg_done, p)

            def cross_stage(pos, p):
                if pos == 0:
                    act.wait_ge(k1_proj.sem, k1_proj.at(p, 1))
                    S.activation(k1[:].rearrange("q c t -> q (c t)"), cross[:], ACT.Copy).then_inc(k1_ready.sem, 1)
                if pos == 1:
                    act.wait_ge(v1_proj.sem, v1_proj.at(p, 1))
                    S.activation(v1[:, :, :, 0:DH1], cross[:].rearrange("q (b n d) -> q b n d", b=PAIR, d=DH1),
                                 ACT.Copy).then_inc(v1_ready.sem, 1)
                    act.wait_ge(mv3_done.sem, mv3_done.at(p, 1))
                    rsqrt(mv3[:, :, 1], rs3[:], 1.0, lg3, rs3_done, p)
                if pos == 3:
                    act.wait_ge(xh3_turned.sem, xh3_turned.at(p, 1))
                    S.activation(xh3T[:].rearrange("q c t -> q (c t)"), cross[:], ACT.Copy).then_inc(xh3T_ready.sem, 1)
                if pos == 4:
                    act.wait_ge(q1_proj.sem, q1_proj.at(p, 1))
                    for c in range(KC):
                        for par in range(2):
                            last = S.activation(q1[:, c, par, :], cross[:, c * T2:(c + 1) * T2], ACT.Identity,
                                                bias=qb1[:, c, par:par + 1], scale=half32[:, par:par + 1])
                    last.then_inc(q1_ready.sem, 1)
                v, r = divmod(pos - 5, 3)
                if pos >= 5 and r == 0 and v < UC:
                    act.wait_ge(scored3.sem, scored3.at(p, v + 1))
                    S.activation(sc3[:, 0, :], cross[:], ACT.Copy).then_inc(copied3.sem, 1)
                if pos >= 5 and r == 2 and v < UC:
                    act.wait_ge(turned3.sem, turned3.at(p, v + 1))
                    S.activation(e3[:, 0, :], cross[:], ACT.Exp).then_inc(exp3.sem, 1)
                if pos == 19:
                    act.wait_ge(co_turned.sem, co_turned.at(p, 1))
                    S.activation(coT[:].rearrange("q c t -> q (c t)"), cross[:], ACT.Copy).then_inc(coT_ready.sem, 1)

            def body(i, on):
                for pos in range(POS):
                    if on[0]:
                        attention(pos, i)
                    if on[1]:
                        ffn_stage(pos, i - 1)
                    if on[0]:
                        attention_root(pos, i)
                    if on[2]:
                        mamba_stage(pos, i - 2)
                    if on[0]:
                        attention_effect(pos, i)
                    if on[3]:
                        cross_stage(pos, i - 3)
            run(act, body)

        @block.vector
        def _(dve):
            V = nc.vector
            dve.wait_ge(loaded.sem, ALL_LOADED)
            dve.wait_ge(set_up.sem, 5)
            n = [5]

            def step(ins):
                n[0] += 1
                ins.then_inc(set_up.sem, 1)
                dve.wait_ge(set_up.sem, n[0])

            step(V.memset(minus[:].bitcast(F32), -1.0))
            V.tensor_copy(identb[:], ident[:])
            V.tensor_copy(causal[:].rearrange("q (n k) -> q n k", n=4), later[:].unsqueeze(1).broadcast_to([P, 4, P]))
            step(V.tensor_scalar(gam[:], gam[:], 0.0, None, ALU.max))
            step(V.tensor_tensor(gam[:], gam[:], gabs[:], ALU.add))
            step(V.tensor_tensor(gam[:], gam[:], gam[:], ALU.mult))
            gview = gam[:].rearrange("q (c j e) -> q j c e", c=2, j=4, e=2)
            for j in range(4):
                for c in range(2):
                    step(V.tensor_tensor(distg[:, j, c, :, :], dist[:].unsqueeze(1).broadcast_to([P, 2, P]),
                                         gview[:, j, c, :].unsqueeze(2).broadcast_to([P, 2, P]), ALU.mult))
            step(V.tensor_scalar(nega[:], nega[:], -1.0, None, ALU.mult))
            step(V.tensor_copy(padmask[:, 0:P], mask8[:]))
            for m in range(1, 4):
                step(V.tensor_scalar(padmask[:, m * P:(m + 1) * P], padmask[:, 0:P], -1e30, None, ALU.mult))
            step(V.tensor_copy(padmask[:, 0:P], padmask[:, P:2 * P]))
            for c in range(KC):
                for par in range(2):
                    step(V.tensor_tensor(qb0[:, c, par:par + 1], bk0[:, c:c + 1], half16[:, par:par + 1], ALU.mult))
            step(V.tensor_tensor(ln1b_r[:], ln1b_r[:], b2_r[:], ALU.add))
            for c in range(KC):
                step(V.tensor_scalar(win[:, c, :], win[:, c, :], nw_c[:, c:c + 1], None, ALU.mult))
            for c in range(DI // P):
                step(V.tensor_scalar(wout[:, c, :], wout[:, c, :], gw_c[:, c:c + 1], None, ALU.mult))
            n[0] += 1
            dve.wait_ge(set_up.sem, n[0])
            for c in range(KC):
                for par in range(2):
                    step(V.tensor_tensor(qb1[:, c, par:par + 1], cross[:, c:c + 1], half32[:, par:par + 1], ALU.mult))
            for c in range(KC):
                step(V.tensor_scalar(wq1[:, c, :], wq1[:, c, :], lw_c[:, c:c + 1], None, ALU.mult))
            assert n[0] == SETUP_DONE, n

            def moments(x_, st, mv, st_sig, mv_sig, p):
                for b in range(PAIR):
                    last = V.bn_stats(st[:, b, :], x_[:, b, :])
                last.then_inc(st_sig.sem, 1)
                dve.wait_ge(loaded.sem, ALL_LOADED)
                dve.wait_ge(st_sig.sem, st_sig.at(p, 1))
                for b in range(PAIR):
                    last = V.bn_aggr(mv[:, b, :], st[:, b, :])
                last.then_inc(mv_sig.sem, 1)

            def centre(o, x_, mv, rs, done):
                for b in range(PAIR):
                    last = V.tensor_scalar(o[:, b, :], x_[:, b, :], mv[:, b, 0:1], rs[:, b:b + 1],
                                           ALU.subtract, ALU.mult)
                last.then_inc(done.sem, 1)

            def heads(ap):
                return ap.rearrange("q (n k) -> q n k", n=4)

            def attention(pos, p):
                s = pos // 2
                if pos == 0:
                    dve.wait_ge(k_proj.sem, k_proj.at(p, 1))
                    for c in range(KC):
                        last = V.tensor_scalar(k0[:, c, :], turned[:, c * T2:(c + 1) * T2], bk0[:, c:c + 1], None, ALU.add)
                    last.then_inc(k_ready.sem, 1)
                    dve.wait_ge(v_proj.sem, v_proj.at(p, 1))
                    V.tensor_tensor(v0[:, :, :, 0:DH0], sums[:].rearrange("q (b n d) -> q b n d", b=PAIR, d=DH0),
                                    bv_r[:].rearrange("q (n d) -> q n d", d=DH0).unsqueeze(1).broadcast_to([P, PAIR, H0, DH0]),
                                    ALU.add).then_inc(v_ready.sem, 1)
                if pos % 2 == 0 and s < UA:
                    dve.wait_ge(copied.sem, copied.at(p, s + 1))
                    dve.wait_ge(diag1.sem, diag1.at(p, s - 1))
                    V.tensor_reduce(m1[:, s % 2, :], heads(sc0[:, s % 4, :]), AX, ALU.max).then_inc(maxed.sem, 1)

            def attention_late(pos, p):
                s = pos // 2
                u = s - 2
                if pos % 2 == 0 and 0 <= u < UA:
                    dve.wait_ge(effect.sem, effect.at(p, u + 1))
                    V.scalar_tensor_tensor(dec0[:, u % 2, :], dec0[:, u % 2, :], 1e-5, sc0[:, u % 4, :],
                                           ALU.max, ALU.mult).then_inc(decayed.sem, 1)
                    dve.wait_ge(decayed.sem, decayed.at(p, u + 1))
                    dve.wait_ge(diag2.sem, diag2.at(p, u - 1))
                    V.tensor_reduce(m2[:, u % 2, :], heads(dec0[:, u % 2, :]), AX, ALU.max).then_inc(maxed2.sem, 1)
                u = s - 3
                if pos % 2 == 1 and 0 <= u < UA and u % 4 == 3:
                    b = u // 4
                    o = attn_out[:, 0:H0 * (DH0 + 1)].rearrange("q (n d) -> q n d", d=DH0 + 1)
                    dve.wait_ge(weighed.sem, weighed.at(p, u + 1))
                    V.reciprocal(rz2[:], o[:, :, DH0]).then_inc(recip2.sem, 1)
                    dve.wait_ge(recip2.sem, recip2.at(p, b + 1))
                    dve.wait_ge(att_turned.sem, att_turned.at(p - 1, 1))
                    V.tensor_tensor(att[:, b, :].rearrange("q (n d) -> q n d", d=DH0), o[:, :, 0:DH0],
                                    rz2[:].unsqueeze(2).broadcast_to([P, H0, DH0]), ALU.mult).then_inc(att_ready.sem, 1)
                u = s - 1
                if pos % 2 == 1 and 0 <= u < UA:
                    dve.wait_ge(summed.sem, summed.at(p, u + 1))
                    dve.wait_ge(normed.sem, normed.at(p, u - 1))
                    dve.wait_ge(turned2.sem, turned2.at(p, u - 1))
                    V.reciprocal(rz[:, u % 2, :], heads(sums[:])[:, :, P - 1]).then_inc(recip1.sem, 1)
                    V.scalar_tensor_tensor(dec0[:, u % 2, :], sums[:], 0.0,
                                           distg[:, u % 4, :, :, :].rearrange("q c e k -> q (c e k)"),
                                           ALU.max, ALU.mult).then_inc(distanced.sem, 1)

            def ffn_stage(pos, p):
                if pos == 1:
                    dve.wait_ge(wo_done.sem, wo_done.at(p, 1))
                    dve.wait_ge(xb_ready.sem, xb_ready.at(p, 1))
                    V.tensor_tensor(s1[:].rearrange("q b d -> q (b d)"), ffn[:], xb[:].rearrange("q b d -> q (b d)"),
                                    ALU.add).then_inc(s1_done.sem, 1)
                    dve.wait_ge(s1_done.sem, s1_done.at(p, 1))
                    moments(s1, st1, mv1, st1_done, mv1_done, p)
                if pos == 3:
                    dve.wait_ge(rs1_done.sem, rs1_done.at(p, 1))
                    dve.wait_ge(x1b_ready.sem, x1b_ready.at(p - 1, 1))
                    centre(s1, s1, mv1, rs1, xh1_ready)
                if pos in (6, 8):
                    n_ = pos - 5
                    dve.wait_ge(up_done.sem, up_done.at(p, n_ + 1))
                    for c in range(2):
                        m = 2 * n_ + c
                        last = V.tensor_scalar(hT[:, m, :], ffn[:, c * T2:(c + 1) * T2], b1[:, m:m + 1], 0.0,
                                               ALU.add, ALU.max)
                    last.then_inc(relu_v.sem, 1)
                if pos == 12:
                    dve.wait_ge(down_done.sem, down_done.at(p, 1))
                    dve.wait_ge(x1b_ready.sem, x1b_ready.at(p, 1))
                    V.tensor_tensor(s1[:].rearrange("q b d -> q (b d)"), ffn[:], x1b[:].rearrange("q b d -> q (b d)"),
                                    ALU.add).then_inc(s2_done.sem, 1)
                    dve.wait_ge(s2_done.sem, s2_done.at(p, 1))
                    moments(s1, st2, mv2, st2_done, mv2_done, p)
                if pos == 14:
                    dve.wait_ge(rs2_done.sem, rs2_done.at(p, 1))
                    dve.wait_ge(x2_ready.sem, x2_ready.at(p - 1, 1))
                    centre(s1, s1, mv2, rs2, xh2_ready)
                if pos == 17:
                    dve.wait_ge(rsr_done.sem, rsr_done.at(p, 1))
                    for b in range(PAIR):
                        last = V.tensor_scalar(s1[:, b, :], x2[:, b, :], ms[:, b:b + 1], None, ALU.mult)
                    last.then_inc(xn_ready.sem, 1)

            def mamba_stage(pos, p):
                if pos == 0:
                    dve.wait_ge(x2_ready.sem, x2_ready.at(p, 1))
                    dve.wait_ge(h_ready.sem, h_ready.at(p - 1, 1))
                    V.tensor_copy(resid[:], x2[:]).then_inc(resid_ready.sem, 1)
                if 1 <= pos < 4:
                    c = pos - 1
                    dve.wait_ge(conv_in.sem, conv_in.at(p, c + 1))
                    for k in range(TAPS - 1):
                        for n_, m in enumerate(range(*CHUNKS[c])):
                            if k:
                                dve.wait_ge(tap_done.sem, tap_done.at(p, 6 * c + 2 * k + n_ - 1))
                            o = acc[:, m, :].rearrange("q (b t) -> q b t", b=PAIR)
                            V.scalar_tensor_tensor(o, cin[:, m, :, k:k + P], convw[:, m, k:k + 1], o,
                                                   ALU.mult, ALU.add).then_inc(tap_done.sem, 1)
                if pos == 3:
                    dve.wait_ge(dt_done.sem, dt_done.at(p, 1))
                    V.tensor_scalar(dtv[:], mamba[1][0:HM, 0:T2], dtb[:], None, ALU.add).then_inc(dt_raw.sem, 1)
                    dve.wait_ge(dt_raw.sem, dt_raw.at(p, 1))
                    V.tensor_scalar(dtp[:], dtv[:], 0.0, None, ALU.max).then_inc(dt_pos.sem, 1)
                if 3 <= pos < 6:
                    lo, hi = CHUNKS[pos - 3]
                    dve.wait_ge(esig_done.sem, esig_done.at(p, pos - 2))
                    V.tensor_scalar(esig[:, 2 * lo:2 * hi, :], esig[:, 2 * lo:2 * hi, :], SIG_MAX, None, ALU.min).then_inc(eclip.sem, 1)
                if pos == 5:
                    dve.wait_ge(dt_log.sem, dt_log.at(p, 1))
                    dve.wait_ge(dt_pos.sem, dt_pos.at(p, 1))
                    V.tensor_tensor(sp[:], dtp[:], dta[:], ALU.add).then_inc(sp_ready.sem, 1)
                if pos in (5, 6):
                    b = pos - 5
                    dve.wait_ge(z_exp.sem, z_exp.at(p, b + 1))
                    V.tensor_scalar(ez[:, b, :], ez[:, b, :], SIG_MAX, None, ALU.min).then_inc(z_clip.sem, 1)
                if 5 <= pos < 8:
                    lo, hi = CHUNKS[pos - 5]
                    dve.wait_ge(sigm.sem, sigm.at(p, pos - 4))
                    V.tensor_tensor(acc_v[:, 2 * lo:2 * hi, :], acc_v[:, 2 * lo:2 * hi, :], esig[:, 2 * lo:2 * hi, :], ALU.mult).then_inc(xc_ready.sem, 1)
                if pos in (6, 7, 9, 10):
                    k = (6, 7, 9, 10).index(pos)
                    dve.wait_ge(spread.sem, spread.at(p, k + 1))
                    V.tensor_tensor_scan(g[:, k // 2, (k % 2) * 512:(k % 2 + 1) * 512], mamba[MB[pos]][:], eye4[:], 0.0,
                                         ALU.mult, ALU.add).then_inc(scanned.sem, 1)
                if pos in (9, 11):
                    b = (pos - 9) // 2
                    dve.wait_ge(scanned.sem, scanned.at(p, 2 * b + 2))
                    dve.wait_ge(cb_ready.sem, cb_ready.at(p, 1))
                    gb = g[:, b, :].rearrange("q (n t) -> q n t", t=P)
                    V.tensor_tensor(gb, gb, cbdt[:, b * P:(b + 1) * P].unsqueeze(1).broadcast_to([P, HM, P]),
                                    ALU.mult).then_inc(mixed.sem, 1)
                if pos in (12, 13):
                    b = pos - 12
                    dve.wait_ge(x_turned.sem, x_turned.at(p, b + 1))
                    xt = mamba[MB[pos]][:].rearrange("q (n d) -> q n d", d=HD)
                    V.tensor_tensor(dtx[:, b, :].rearrange("q (n d) -> q n d", d=HD), xt,
                                    cbdt[:, 2 * P + b * HM:2 * P + (b + 1) * HM].unsqueeze(2).broadcast_to([P, HM, HD]),
                                    ALU.mult)
                    V.tensor_tensor(y[:, b, :].rearrange("q (n d) -> q n d", d=HD), xt,
                                    dskip_r[:].unsqueeze(2).broadcast_to([P, HM, HD]), ALU.mult).then_inc(xtok.sem, 1)
                if pos in (14, 15):
                    b = pos - 14
                    dve.wait_ge(y_done.sem, y_done.at(p, b + 1))
                    V.tensor_tensor(y[:, b, :], mamba[MB[pos]][:], y[:, b, :], ALU.add).then_inc(y_skip.sem, 1)
                    dve.wait_ge(y_skip.sem, y_skip.at(p, b + 1))
                    dve.wait_ge(zs_ready.sem, zs_ready.at(p, b + 1))
                    V.tensor_tensor(y[:, b, :], y[:, b, :], zs[:, b, :], ALU.mult).then_inc(y_gated.sem, 1)
                if pos == 20:
                    dve.wait_ge(mout_done.sem, mout_done.at(p, 1))
                    dve.wait_ge(rsg_done.sem, rsg_done.at(p, 1))
                    for b in range(PAIR):
                        last = V.scalar_tensor_tensor(h[:, b, :], mamba[1][:, b * D:(b + 1) * D], ssq[:, b:b + 1],
                                                      resid[:, b, :], ALU.mult, ALU.add)
                    last.then_inc(h_ready.sem, 1)

            def cross_stage(pos, p):
                if pos == 0:
                    dve.wait_ge(h_ready.sem, h_ready.at(p, 1))
                    dve.wait_ge(out_ready.sem, out_ready.at(p - 1, 1))
                    V.tensor_copy(hres[:], h[:]).then_inc(hres_ready.sem, 1)
                    moments(h, st3, mv3, st3_done, mv3_done, p)
                if pos == 2:
                    dve.wait_ge(rs3_done.sem, rs3_done.at(p, 1))
                    dve.wait_ge(hres_ready.sem, hres_ready.at(p, 1))
                    centre(h, h, mv3, rs3, xh3_ready)
                v, r = divmod(pos - 5, 3)
                if pos >= 5 and r == 0 and v < UC:
                    dve.wait_ge(copied3.sem, copied3.at(p, v + 1))
                    V.tensor_reduce(m3[:, v % 2, :], heads(sc3[:, 0, :]), AX, ALU.max).then_inc(maxed3.sem, 1)
                v, r = divmod(pos - 9, 3)
                if pos >= 9 and r == 0 and v < UC:
                    b, jj = divmod(v, 2)
                    o = cross[:, 0:4 * (DH1 + 1)].rearrange("q (c e d) -> q c e d", c=2, e=2)
                    dve.wait_ge(weighed3.sem, weighed3.at(p, v + 1))
                    dve.wait_ge(co_ready.sem, co_ready.at(p, v))
                    dve.wait_ge(stored.sem, stored.at(p, 0))
                    V.reciprocal(rz3[:].rearrange("q (c e) -> q c e", c=2), o[:, :, :, DH1]).then_inc(recip3.sem, 1)
                    dve.wait_ge(recip3.sem, recip3.at(p, v + 1))
                    V.tensor_tensor(co[:, b, :].rearrange("q (c j e d) -> q j c e d", c=2, j=2, e=2)[:, jj, :, :, :],
                                    o[:, :, :, 0:DH1],
                                    rz3[:].rearrange("q (c e) -> q c e", c=2).unsqueeze(3).broadcast_to([P, 2, 2, DH1]),
                                    ALU.mult).then_inc(co_ready.sem, 1)
                if pos == 21:
                    dve.wait_ge(out_proj.sem, out_proj.at(p, 1))
                    V.tensor_tensor(res[:].rearrange("q b d -> q (b d)"), cross[:], hres[:].rearrange("q b d -> q (b d)"),
                                    ALU.add).then_inc(out_ready.sem, 1)

            def body(i, on):
                for pos in range(POS):
                    if on[0]:
                        attention(pos, i)
                    if on[1]:
                        ffn_stage(pos, i - 1)
                    if on[2]:
                        mamba_stage(pos, i - 2)
                    if on[3]:
                        cross_stage(pos, i - 3)
                    if on[0]:
                        attention_late(pos, i)
            run(dve, body)

        @block.tensor
        def _(pe):
            M = nc.tensor
            pe.wait_ge(loaded.sem, ALL_LOADED)
            pe.wait_ge(set_up.sem, SETUP_DONE - 7)
            for c in range(KC):
                for k in range(KC):
                    last = M.matmul(cross[:, c:c + 1], wq1[:, k, c * P:(c + 1) * P], lb_c[:, k:k + 1],
                                    start=(k == 0), stop=(k == KC - 1))
            last.then_inc(set_up.sem, 1)
            pe.wait_ge(set_up.sem, SETUP_DONE)

            def project(bank_, w, xt):
                for c in range(KC):
                    for k in range(KC):
                        last = M.matmul(bank_[:, c * T2:(c + 1) * T2], w[:, k, c * P:(c + 1) * P], xt[:, k, :],
                                        start=(k == 0), stop=(k == KC - 1))
                return last

            def project_tokens(bank_, xt, w, chunks=KC):
                for b in range(PAIR):
                    for k in range(chunks):
                        last = M.matmul(bank_[:, b * D:(b + 1) * D], xt(k, b), w[:, k, :],
                                        start=(k == 0), stop=(k == chunks - 1))
                return last

            def turn(bank_, src):
                for c in range(KC):
                    for b in range(PAIR):
                        last = M.transpose(bank_[:, c * T2 + b * P:c * T2 + (b + 1) * P],
                                           src[:, b, c * P:(c + 1) * P], ident[:])
                return last

            def turn_less_max(bank_, src, dg):
                for n_ in range(4):
                    M.matmul(bank_[:, n_ * P:(n_ + 1) * P], src[:, n_ * P:(n_ + 1) * P], ident[:],
                             start=(n_ == 0), stop=False, is_transpose=True, skip_group_check=True)
                return M.matmul(bank_[:], minus[:], dg, start=False, stop=True, skip_group_check=True)

            def masked_scores(bank_, mask, q, k, r0, nrow, b):
                M.matmul(bank_[:], identb[:], mask[:], start=True, stop=False, skip_group_check=True)
                for c in range(KC):
                    for par in range(2):
                        n_ = 2 * c + par
                        last = M.matmul(bank_[:, n_ * P:(n_ + 1) * P], q[r0:r0 + nrow, c, par, b * P:(b + 1) * P],
                                        k[r0:r0 + nrow, c, b * P:(b + 1) * P], start=False, stop=True,
                                        skip_group_check=True)
                return last

            def attention(pos, p):
                s = pos // 2
                if pos == 0:
                    pe.wait_ge(a_loaded.sem, a_loaded.at(p, 32))
                    project(scores, wk0, xT).then_inc(q_proj.sem, 1)
                    pe.wait_ge(exp2.sem, exp2.at(p, 0))
                    project(turned, wk0, cT).then_inc(k_proj.sem, 1)
                    project_tokens(sums, lambda k, b: cT[:, k, b * P:(b + 1) * P], wv0).then_inc(v_proj.sem, 1)
                if pos % 2 == 0:
                    if 0 <= s - 3 < UA:
                        u = s - 3
                        pe.wait_ge(exp1.sem, exp1.at(p, min(u + 2, UA)))
                        pe.wait_ge(diag2.sem, diag2.at(p, u + 1))
                        turn_less_max(turned, dec0[:, u % 2, :], dg2[:, u % 2, :]).then_inc(turned2.sem, 1)
                    if s < UA:
                        if s == 0:
                            pe.wait_ge(q_ready.sem, q_ready.at(p, 1))
                            pe.wait_ge(k_ready.sem, k_ready.at(p, 1))
                        pe.wait_ge(copied.sem, copied.at(p, s))
                        masked_scores(scores, causal, q0, k0, 32 * (s % 4), 32, s // 4).then_inc(scored.sem, 1)
                else:
                    if 0 <= s - 3 < UA:
                        u = s - 3
                        b, j = divmod(u, 4)
                        pe.wait_ge(exp2.sem, exp2.at(p, u + 1))
                        if j == 0:
                            pe.wait_ge(att_ready.sem, att_ready.at(p, b))
                        for n_ in range(4):
                            hd = 8 * (n_ // 2) + 2 * j + n_ % 2
                            last = M.matmul(attn_out[:, hd * (DH0 + 1):(hd + 1) * (DH0 + 1)],
                                            e1[:, u % 2, n_ * P:(n_ + 1) * P], v0[:, b, hd, :], start=True, stop=True)
                        last.then_inc(weighed.sem, 1)
                    if 0 <= s - 1 < UA:
                        u = s - 1
                        pe.wait_ge(copied.sem, copied.at(p, u + 1))
                        pe.wait_ge(diag1.sem, diag1.at(p, u + 1))
                        pe.wait_ge(exp1.sem, exp1.at(p, u))
                        if u >= 2:
                            pe.wait_ge(exp2.sem, exp2.at(p, u - 1))
                        turn_less_max(turned, sc0[:, u % 4, :], dg1[:, u % 2, :]).then_inc(turned1.sem, 1)

            def attention_late(pos, p):
                u = pos // 2 - 1
                if pos % 2 == 1 and 0 <= u < UA:
                    pe.wait_ge(exp1.sem, exp1.at(p, u + 1))
                    if u == 0:
                        pe.wait_ge(v_ready.sem, v_ready.at(p, 1))
                    pe.wait_ge(distanced.sem, distanced.at(p, u))
                    for n_ in range(4):
                        last = M.matmul(sums[:, n_ * P:(n_ + 1) * P], e0[:, u % 2, n_ * P:(n_ + 1) * P], tri[:],
                                        start=True, stop=True)
                    last.then_inc(summed.sem, 1)

            def ffn_stage(pos, p):
                if pos == 0:
                    pe.wait_ge(att_ready.sem, att_ready.at(p, PAIR))
                    pe.wait_ge(xnT_ready.sem, xnT_ready.at(p - 1, 1))
                    turn(ffn, att).then_inc(att_turned.sem, 1)
                if pos == 1:
                    pe.wait_ge(attT_ready.sem, attT_ready.at(p, 1))
                    project_tokens(ffn, lambda k, b: attT[:, k, b * P:(b + 1) * P], wo0).then_inc(wo_done.sem, 1)
                if pos == 4:
                    pe.wait_ge(xh1_ready.sem, xh1_ready.at(p, 1))
                    turn(ffn, s1).then_inc(x1_turned.sem, 1)
                if 5 <= pos < 9:
                    n_ = pos - 5
                    pe.wait_ge(x1T_ready.sem, x1T_ready.at(p, 1))
                    pe.wait_ge(relu_a.sem, relu_a.at(p, (n_ + 1) // 2))
                    pe.wait_ge(relu_v.sem, relu_v.at(p, n_ // 2))
                    for c in range(2):
                        for k in range(KC):
                            last = M.matmul(ffn[:, c * T2:(c + 1) * T2],
                                            w1[:, k, (2 * n_ + c) * P:(2 * n_ + c + 1) * P],
                                            x1T[:, k, :], start=(k == 0), stop=(k == KC - 1))
                    last.then_inc(up_done.sem, 1)
                if pos in (10, 12):
                    b = (pos - 10) // 2
                    pe.wait_ge(relu_a.sem, relu_a.at(p, 2))
                    pe.wait_ge(relu_v.sem, relu_v.at(p, 2))
                    for k in range(FM):
                        last = M.matmul(ffn[:, b * D:(b + 1) * D], hT[:, k, b * P:(b + 1) * P], w2[:, k, :],
                                        start=(k == 0), stop=(k == FM - 1))
                    if b:
                        last.then_inc(down_done.sem, 1)
                if pos == 18:
                    pe.wait_ge(xn_ready.sem, xn_ready.at(p, 1))
                    turn(ffn, s1).then_inc(xn_turned.sem, 1)

            def mamba_stage(pos, p):
                if pos < 3:
                    lo, hi = CHUNKS[pos]
                    if pos == 0:
                        pe.wait_ge(xnT_ready.sem, xnT_ready.at(p, 1))
                        pe.wait_ge(yT_ready.sem, yT_ready.at(p - 1, PAIR))
                    elif pos == 1:
                        pe.wait_ge(h_ready.sem, h_ready.at(p - 1, 1))
                    else:
                        pe.wait_ge(conv_in.sem, conv_in.at(p, 1))
                    for n_, m in enumerate(range(lo, hi)):
                        for k in range(KC):
                            last = M.matmul(mamba[pos % 2][:, n_ * T2:(n_ + 1) * T2],
                                            win[:, k, DI + m * P:DI + (m + 1) * P], xnT[:, k, :],
                                            start=(k == 0), stop=(k == KC - 1))
                    last.then_inc(xbc_done.sem, 1)
                if pos == 3:
                    pe.wait_ge(conv_in.sem, conv_in.at(p, 2))
                    for k in range(KC):
                        last = M.matmul(mamba[1][0:HM, 0:T2], win[:, k, 2 * DI + 2 * P:2 * DI + 2 * P + HM], xnT[:, k, :],
                                        start=(k == 0), stop=(k == KC - 1))
                    last.then_inc(dt_done.sem, 1)
                if pos in (4, 5):
                    b = pos - 4
                    if b == 0:
                        pe.wait_ge(conv_in.sem, conv_in.at(p, 3))
                    else:
                        pe.wait_ge(dt_raw.sem, dt_raw.at(p, 1))
                    for k in range(KC):
                        last = M.matmul(mamba[b][:], xnT[:, k, b * P:(b + 1) * P], win[:, k, 0:DI],
                                        start=(k == 0), stop=(k == KC - 1))
                    last.then_inc(z_done.sem, 1)
                if pos in (6, 7, 9, 10):
                    n_ = (6, 7, 9, 10).index(pos)
                    pe.wait_ge(decay_ready.sem, decay_ready.at(p, 1))
                    if pos in (6, 7):
                        pe.wait_ge(z_exp.sem, z_exp.at(p, pos - 5))
                    elif pos == 9:
                        pe.wait_ge(scanned.sem, scanned.at(p, 2))
                    else:
                        pe.wait_ge(cb_ready.sem, cb_ready.at(p, 1))
                    for m in range(4):
                        last = M.matmul(mamba[MB[pos]][:, m * P:(m + 1) * P], ident[0:HM, 4 * (n_ % 2) + m:4 * (n_ % 2) + m + 1].broadcast_to([HM, P]),
                                        decay[:, n_ // 2, :], start=True, stop=True)
                    last.then_inc(spread.sem, 1)
                if pos == 8:
                    pe.wait_ge(xc_ready.sem, xc_ready.at(p, 1))
                    pe.wait_ge(scanned.sem, scanned.at(p, 1))
                    pe.wait_ge(sp_ready.sem, sp_ready.at(p, 1))
                    for b in range(PAIR):
                        M.matmul(mamba[0][:, b * P:(b + 1) * P], xc[:, 4, b * P:(b + 1) * P],
                                 xc[:, 5, b * P:(b + 1) * P], start=True, stop=True)
                    for b in range(PAIR):
                        last = M.transpose(mamba[0][:, 2 * P + b * HM:2 * P + (b + 1) * HM], sp[:, b * P:(b + 1) * P],
                                           ident[0:HM, 0:HM])
                    last.then_inc(cb_done.sem, 1)
                if pos in (12, 13):
                    b = pos - 12
                    pe.wait_ge(xc_ready.sem, xc_ready.at(p, 3))
                    pe.wait_ge(scanned.sem, scanned.at(p, 3 + b))
                    for c in range(DI // P):
                        last = M.transpose(mamba[MB[pos]][:, c * P:(c + 1) * P], xc[:, c, b * P:(b + 1) * P], ident[:])
                    last.then_inc(x_turned.sem, 1)
                if pos in (14, 15):
                    b = pos - 14
                    pe.wait_ge(mixed.sem, mixed.at(p, b + 1))
                    pe.wait_ge(xtok.sem, xtok.at(p, b + 1))
                    for n_ in range(HM):
                        last = M.matmul(mamba[MB[pos]][:, n_ * HD:(n_ + 1) * HD], g[:, b, n_ * P:(n_ + 1) * P],
                                        dtx[:, b, n_ * HD:(n_ + 1) * HD], start=True, stop=True)
                    last.then_inc(y_done.sem, 1)
                if pos in (17, 18):
                    b = pos - 17
                    pe.wait_ge(y_gated.sem, y_gated.at(p, b + 1))
                    for c in range(DI // P):
                        last = M.transpose(mamba[(b + 1) % 2][:, c * P:(c + 1) * P], y[:, b, c * P:(c + 1) * P], ident[:])
                    last.then_inc(y_turned.sem, 1)
                if pos == 20:
                    pe.wait_ge(yT_ready.sem, yT_ready.at(p, PAIR))
                    project_tokens(mamba[1], lambda k, b: yT[:, b, k * P:(k + 1) * P], wout,
                                   DI // P).then_inc(mout_done.sem, 1)

            def cross_stage(pos, p):
                if pos == 0:
                    pe.wait_ge(c_loaded.sem, c_loaded.at(p, 16))
                    pe.wait_ge(out_ready.sem, out_ready.at(p - 1, 1))
                    project(cross, wk1, cTc).then_inc(k1_proj.sem, 1)
                if pos == 1:
                    pe.wait_ge(k1_ready.sem, k1_ready.at(p, 1))
                    project_tokens(cross, lambda k, b: cTc[:, k, b * P:(b + 1) * P], wv1).then_inc(v1_proj.sem, 1)
                if pos == 3:
                    pe.wait_ge(xh3_ready.sem, xh3_ready.at(p, 1))
                    pe.wait_ge(v1_ready.sem, v1_ready.at(p, 1))
                    turn(cross, h).then_inc(xh3_turned.sem, 1)
                if pos == 4:
                    pe.wait_ge(xh3T_ready.sem, xh3T_ready.at(p, 1))
                    project(cross, wq1, xh3T).then_inc(q1_proj.sem, 1)
                v, r = divmod(pos - 5, 3)
                if pos >= 5 and r == 0 and v < UC:
                    if v == 0:
                        pe.wait_ge(q1_ready.sem, q1_ready.at(p, 1))
                    pe.wait_ge(exp3.sem, exp3.at(p, v))
                    pe.wait_ge(co_ready.sem, co_ready.at(p, max(v - 1, 0)))
                    masked_scores(cross, padmask, q1, k1, 64 * (v % 2), 64, v // 2).then_inc(scored3.sem, 1)
                if pos >= 5 and r == 2 and v < UC:
                    pe.wait_ge(diag3.sem, diag3.at(p, v + 1))
                    pe.wait_ge(copied3.sem, copied3.at(p, v + 1))
                    pe.wait_ge(co_ready.sem, co_ready.at(p, v))
                    turn_less_max(cross, sc3[:, 0, :], dg3[:, 0, :]).then_inc(turned3.sem, 1)
                v, r = divmod(pos - 9, 3)
                if pos >= 9 and r == 0 and v < UC:
                    b, jj = divmod(v, 2)
                    pe.wait_ge(exp3.sem, exp3.at(p, v + 1))
                    pe.wait_ge(copied3.sem, copied3.at(p, min(v + 2, UC)))
                    for n_ in range(4):
                        hd = 4 * (n_ // 2) + 2 * jj + n_ % 2
                        last = M.matmul(cross[:, n_ * (DH1 + 1):(n_ + 1) * (DH1 + 1)],
                                        e3[:, 0, n_ * P:(n_ + 1) * P], v1[:, b, hd, :], start=True, stop=True)
                    last.then_inc(weighed3.sem, 1)
                if pos == 19:
                    pe.wait_ge(co_ready.sem, co_ready.at(p, UC))
                    turn(cross, co).then_inc(co_turned.sem, 1)
                if pos == 20:
                    pe.wait_ge(coT_ready.sem, coT_ready.at(p, 1))
                    project_tokens(cross, lambda k, b: coT[:, k, b * P:(b + 1) * P], wo1).then_inc(out_proj.sem, 1)

            def body(i, on):
                for pos in range(POS):
                    if on[0]:
                        attention(pos, i)
                    if on[1]:
                        ffn_stage(pos, i - 1)
                    if on[2]:
                        mamba_stage(pos, i - 2)
                    if on[3]:
                        cross_stage(pos, i - 3)
                    if on[0]:
                        attention_late(pos, i)
            run(pe, body)


MB = {6: 0, 7: 1, 9: 1, 10: 0, 12: 1, 13: 0, 14: 1, 15: 0}
SETUP_DONE = 1 + 4 + 29 + 1 + 6


def layouts(inputs):
    import numpy as np

    def arr(n):
        return np.ascontiguousarray(np.asarray(inputs[n]))

    def chunked(w):
        return np.ascontiguousarray(w.reshape(-1, P, w.shape[1]).transpose(1, 0, 2))

    def column(v):
        return np.ascontiguousarray(v.reshape(-1, P).T)

    x, c = arr("x"), arr("ctx_1024")
    q, k = np.arange(P)[:, None], np.arange(P)[None, :]
    tri = (q > k).astype(np.float32)
    tri[:, P - 1] = 1.0
    f = np.float32
    par = (np.arange(P) // DH0) % 2
    par1 = (np.arange(P) // DH1) % 2
    d = {
        "xT": np.ascontiguousarray(x.reshape(-1, D).T), "cT": np.ascontiguousarray(c.reshape(-1, D).T),
        "x": np.ascontiguousarray(x.transpose(1, 0, 2)),
        "mask": arr("mask_1xS2_bf0").reshape(P),
        "ident": np.eye(P, dtype=f), "tri": tri,
        "later": np.where(k > q, -1e32, 0.0).astype(f),
        "eye4": np.tile(np.eye(P, dtype=f), (1, 4)), "dist": np.maximum(q - k, 0).astype(f),
        "half16": (np.stack([1 - par, par], 1) / np.sqrt(DH0)).astype(f),
        "half32": (np.stack([1 - par1, par1], 1) / np.sqrt(DH1)).astype(f),
    }
    for name, src in (("wk0", "L0_xattn_Wk"), ("wv0", "L0_xattn_Wv"), ("wo0", "L0_xattn_Wo"),
                      ("w1", "L0_xattn_W1"), ("w2", "L0_xattn_W2")):
        d[name] = chunked(arr(src).T)
    for name, src in (("win", "in_proj_w"), ("wout", "out_proj_w"), ("wq1", "Wq"), ("wk1", "Wk"),
                      ("wv1", "Wv"), ("wo1", "Wo")):
        d[name] = chunked(arr("L1_xattn_" + src))
    for name, src in (("bk0", "L0_xattn_bk"), ("b1", "L0_xattn_b1"), ("ln1_w", "L0_xattn_ln1_w"),
                      ("ln1_b", "L0_xattn_ln1_b"), ("m_norm_w", "L1_xattn_m_norm_w"), ("gnorm_w", "L1_xattn_gnorm_w"),
                      ("ca_ln_w", "L1_xattn_ca_ln_w"), ("ca_ln_b", "L1_xattn_ca_ln_b"), ("conv_b", "L1_xattn_conv_b")):
        d[name] = column(arr(src))
    d["conv_w"] = chunked(arr("L1_xattn_conv_w"))
    d["dt_bias"] = arr("L1_xattn_dt_bias").reshape(HM, 1)
    d["A_log"] = arr("L1_xattn_A_log").reshape(HM, 1)
    for name, src in (("bv0", "L0_xattn_bv"), ("bo0", "L0_xattn_bo"), ("b2", "L0_xattn_b2"),
                      ("ln1_w_row", "L0_xattn_ln1_w"), ("ln1_b_row", "L0_xattn_ln1_b"),
                      ("ln2_w_row", "L0_xattn_ln2_w"), ("ln2_b_row", "L0_xattn_ln2_b"), ("D_skip", "L1_xattn_D_skip"),
                      ("gammas", "L0_xattn_gammas")):
        d[name] = arr(src).reshape(-1)
    return d


def kernel(**inputs):
    import numpy as np
    import concourse.bacc as bacc
    from concourse.bass_utils import run_bass_kernel_spmd

    arrays = layouts(inputs)
    nseq = arrays["x"].shape[1]
    nc = bacc.Bacc("TRN2", target_bir_lowering=False, num_devices=1)
    aps = {n: nc.dram_tensor("in_" + n, v.shape, mybir.dt.from_np(v.dtype), kind="ExternalInput").ap()
           for n, v in arrays.items()}
    out = nc.dram_tensor("out", [nseq, P, D], F32, kind="ExternalOutput").ap()
    build(nc, aps, out.rearrange("n t d -> t n d"))
    r = run_bass_kernel_spmd(nc, [{"in_" + n: v for n, v in arrays.items()}], core_ids=[0])
    return np.asarray(r.results[0]["out"])
```

```python
from contextlib import ExitStack

import concourse.bass as bass
from concourse import mybir

F32 = mybir.dt.float32
F32R = mybir.dt.float32r
U8 = mybir.dt.uint8
ALU = mybir.AluOpType
ACT = mybir.ActivationFunctionType
AX = mybir.AxisListType.X

P = 128
PAIR = 2
T2 = PAIR * P
D = 256
KC = D // P
H0, DH0 = 16, 16
F = 1024
FM = F // P
DI = 512
HM, HD = 8, 64
NIN = 2 * DI + 2 * P + HM
DTR = 32 + HM
CM = 6
TAPS = 4
H1, DH1 = 8, 32
EPS = 1e-5
TINY = 1e-19
SIG_MAX = 1e19
POS = 22
QPOS = 16
UA = 8
UC = 4
CHUNKS = [(4, 6), (0, 2), (2, 4)]


class Signal:

    def __init__(self, sem, per_pair):
        self.sem, self.per_pair = sem, per_pair

    def at(self, p, k):
        value = p * self.per_pair + k
        return max(value, 0) if isinstance(value, int) else value


def build(nc, a, out):
    NSEQ = out.shape[1]
    NP = NSEQ // PAIR
    ctx = ExitStack()
    with ctx:
        def sb(name, shape, dt=F32):
            return ctx.enter_context(nc.sbuf_tensor(name, shape, dt))

        def bank(name):
            return ctx.enter_context(nc.psum_tensor(name, [P, 512], F32))

        def sig(name, per_pair):
            return Signal(ctx.enter_context(nc.semaphore(name)), per_pair)

        ident = sb("ident", [P, P])
        later = sb("later", [P, P])
        tri = sb("tri", [P, P])
        padmask = sb("padmask", [P, P])
        eye4 = sb("eye4", [P, 4 * P])
        dist = sb("dist", [P, P])
        half16 = sb("half16", [P, 2])
        half32 = sb("half32", [P, 2])
        wk0 = sb("wk0", [P, KC, D])
        wv0 = sb("wv0", [P, KC, D])
        w2 = sb("w2", [P, FM, D])
        wout = sb("wout", [P, DI // P, D])
        wk1 = sb("wk1", [P, KC, D])
        wv1 = sb("wv1", [P, KC, D])
        win = sb("win", [P, KC, NIN])
        wo0, w1, wq1, wo1 = (
            [sb(n + part, [P, KC, width], F32R) for part in ("_hi", "_lo")]
            for n, width in (("wo0", D), ("w1", F), ("wq1", D), ("wo1", D)))
        wdt = sb("wdt", [P, KC, DTR])
        sel = sb("sel", [DTR, HM], F32R)
        selp = sb("selp", [DTR, HM])
        bk0 = sb("bk0", [P, KC])
        qb0 = sb("qb0", [P, KC, 2])
        qb1 = sb("qb1", [P, KC, 2])
        b1 = sb("b1", [P, FM])
        ln1w_c = sb("ln1w_c", [P, KC])
        ln1b_c = sb("ln1b_c", [P, KC])
        nw_c = sb("nw_c", [P, KC])
        gw_c = sb("gw_c", [P, DI // P])
        lw_c = sb("lw_c", [P, KC])
        lb_c = sb("lb_c", [P, KC])
        convw = sb("convw", [P, CM, TAPS])
        convb = sb("convb", [P, CM])
        dtb = sb("dtb", [DTR, 1])
        nega = sb("nega", [DTR, 1])
        bv_r = sb("bv_r", [P, D])
        bo_r = sb("bo_r", [P, D])
        ln1w_r = sb("ln1w_r", [P, D])
        ln1b_r = sb("ln1b_r", [P, D])
        ln2w_r = sb("ln2w_r", [P, D])
        ln2b_r = sb("ln2b_r", [P, D])
        dskip_r = sb("dskip_r", [P, HM])
        gam = sb("gam", [P, H0])
        gabs = sb("gabs", [P, H0])
        gam2 = sb("gam2", [P, H0])
        mask8 = sb("mask8", [P, P], U8)
        eps_c = sb("eps_c", [P, 1])
        tiny_c = sb("tiny_c", [P, 1])

        xT = sb("xT", [P, KC, T2])
        cT = sb("cT", [P, KC, T2])
        q0 = sb("q0", [P, KC, 2, T2])
        k0 = sb("k0", [P, KC, T2])
        v0 = sb("v0", [P, PAIR, H0, DH0 + 1])
        sc0 = sb("sc0", [P, 4, 4 * P])
        m1 = sb("m1", [P, 2, 4])
        m2 = sb("m2", [P, 2, 4])
        sm0 = sb("sm0", [P, 2, 4 * P])
        e0 = sb("e0", [P, 2, 4 * P])
        rz = sb("rz", [P, 2, 4])
        dec0 = sb("dec0", [P, 2, 4 * P])
        e1 = sb("e1", [P, 2, 4 * P])
        rz2 = sb("rz2", [P, H0])
        att = sb("att", [P, PAIR, D])
        xin = sb("xin", [P, PAIR, D])
        xb = sb("xb", [P, PAIR, D])
        bT = [sb("bT_hi", [P, KC, T2], F32R), sb("bT_lo", [P, KC, T2], F32R)]
        s1 = sb("s1", [P, PAIR, D])
        st1 = sb("st1", [P, PAIR, 6])
        mv1 = sb("mv1", [P, PAIR, 2])
        rs1 = sb("rs1", [P, PAIR])
        x1b = sb("x1b", [P, PAIR, D])
        hT = sb("hT", [P, FM, T2])
        st2 = sb("st2", [P, PAIR, 6])
        mv2 = sb("mv2", [P, PAIR, 2])
        rs2 = sb("rs2", [P, PAIR])
        x2 = sb("x2", [P, PAIR, D])
        ms = sb("ms", [P, PAIR])
        xnT = sb("xnT", [P, KC, T2])
        resid = sb("resid", [P, PAIR, D])
        cin = sb("cin", [P, CM, PAIR, TAPS - 1 + P])
        esig = cin[:, :, :, TAPS - 1:].rearrange("q m b t -> q (m b) t")
        acc = sb("acc", [P, CM, T2])
        acc_v = acc[:].rearrange("q m (b t) -> q (m b) t", b=PAIR)
        xc = acc
        dtv = sb("dtv", [DTR, T2])
        dtp = sb("dtp", [DTR, T2])
        dta = sb("dta", [DTR, T2])
        sp = sb("sp", [DTR, T2])
        decay = sb("decay", [DTR, PAIR, P])
        decay_p = sb("decay_p", [DTR, PAIR, P], F32R)
        zc = sb("zc", [P, PAIR, DI])
        ez = sb("ez", [P, PAIR, DI])
        zs = ez
        g = sb("g", [P, PAIR, HM * P])
        cbdt = sb("cbdt", [P, 2 * P + PAIR * HM])
        dtx = sb("dtx", [P, PAIR, DI])
        y = sb("y", [P, PAIR, DI])
        sqy = sb("sqy", [P, DI])
        ssq = sb("ssq", [P, PAIR])
        yT = dtx
        h = sb("h", [P, PAIR, D])
        cTc = sb("cTc", [P, KC, T2])
        hres = sb("hres", [P, PAIR, D])
        k1 = sb("k1", [P, KC, T2])
        v1 = sb("v1", [P, PAIR, H1, DH1 + 1])
        st3 = sb("st3", [P, PAIR, 6])
        mv3 = sb("mv3", [P, PAIR, 2])
        rs3 = sb("rs3", [P, PAIR])
        hT1 = [sb("hT1_hi", [P, KC, T2], F32R), sb("hT1_lo", [P, KC, T2], F32R)]
        q1 = sb("q1", [P, KC, 2, T2])
        m3 = sb("m3", [P, 2, 4])
        sc3 = sb("sc3", [P, 1, 4 * P])
        e3 = sb("e3", [P, 1, 4 * P])
        rz3 = sb("rz3", [P, 4])
        co = sb("co", [P, PAIR, D])
        res = co

        scores, turned, sums, attn_out = bank("scores"), bank("turned"), bank("sums"), bank("attn_out")
        ffn = bank("ffn")
        mamba = [bank("mamba0"), bank("mamba1")]
        cross = bank("cross")

        loaded_a, loaded = sig("loaded_a", 0), sig("loaded", 0)
        set_up = sig("set_up", 0)
        a_loaded = sig("a_loaded", 32)
        q_proj, k_proj, v_proj = sig("q_proj", 1), sig("k_proj", 1), sig("v_proj", 1)
        q_ready, k_ready, v_ready = sig("q_ready", 1), sig("k_ready", 1), sig("v_ready", 1)
        scored, maxed, taken = sig("scored", UA), sig("maxed", UA), sig("taken", UA)
        less1, turned1, exp1 = sig("less1", UA), sig("turned1", UA), sig("exp1", UA)
        summed, recip1, distanced = sig("summed", UA), sig("recip1", 2 * UA), sig("distanced", UA)
        normed = sig("normed", UA)
        log_d, root_d, effect = sig("log_d", UA), sig("root_d", UA), sig("effect", UA)
        decayed, maxed2, less2 = sig("decayed", UA), sig("maxed2", UA), sig("less2", UA)
        turned2, exp2, weighed = sig("turned2", UA), sig("exp2", UA), sig("weighed", UA)
        recip2, att_ready = sig("recip2", PAIR), sig("att_ready", PAIR)

        x_loaded, xb_ready = sig("x_loaded", 16), sig("xb_ready", 1)
        att_turned, attT_hi, attT_ready, wo_done = sig("att_turned", 1), sig("attT_hi", 1), sig("attT_ready", 1), sig("wo_done", 1)
        s1_done, st1_done, mv1_done = sig("s1_done", 1), sig("st1_done", 1), sig("mv1_done", 1)
        lg1, rs1_done, xh1_ready = sig("lg1", 1), sig("rs1_done", 1), sig("xh1_ready", 1)
        x1m_done, x1b_ready = sig("x1m_done", 1), sig("x1b_ready", 1)
        x1_turned, x1T_hi, x1T_ready = sig("x1_turned", 1), sig("x1T_hi", 1), sig("x1T_ready", 1)
        up_done, relu_a, relu_v = sig("up_done", 4), sig("relu_a", 2), sig("relu_v", 2)
        down_done = sig("down_done", 1)
        s2_done, st2_done, mv2_done = sig("s2_done", 1), sig("st2_done", 1), sig("mv2_done", 1)
        lg2, rs2_done, xh2_ready = sig("lg2", 1), sig("rs2_done", 1), sig("xh2_ready", 1)
        x2m_done, x2_ready = sig("x2m_done", 1), sig("x2_ready", 1)
        sq_done, lg_r, rsr_done = sig("sq_done", PAIR), sig("lg_r", 1), sig("rsr_done", 1)
        xn_ready, xn_turned, xnT_ready = sig("xn_ready", 1), sig("xn_turned", 1), sig("xnT_ready", 1)

        resid_ready = sig("resid_ready", 1)
        xbc_done, conv_in = sig("xbc_done", 3), sig("conv_in", 3)
        tap_done = sig("tap_done", 18)
        esig_done, eclip, lnsig, sigm = sig("esig_done", 3), sig("eclip", 3), sig("lnsig", 3), sig("sigm", 3)
        xc_ready = sig("xc_ready", 3)
        dt_raw, decay_high, decay_parts = sig("dt_raw", 1), sig("decay_high", 1), sig("decay_parts", 1)
        dt_done, dt_pos, dt_abs = sig("dt_done", 1), sig("dt_pos", 1), sig("dt_abs", 1)
        dt_exp, dt_log, sp_ready, decay_ready = sig("dt_exp", 1), sig("dt_log", 1), sig("sp_ready", 1), sig("decay_ready", 1)
        z_done, z_exp, z_clip, z_log, z_sig, zs_ready = (sig(n, PAIR) for n in (
            "z_done", "z_exp", "z_clip", "z_log", "z_sig", "zs_ready"))
        spread, scanned = sig("spread", 4), sig("scanned", 4)
        cb_done, cb_ready = sig("cb_done", 1), sig("cb_ready", 1)
        mixed, x_turned, xtok = sig("mixed", PAIR), sig("x_turned", PAIR), sig("xtok", PAIR)
        y_done, y_skip, y_gated, ysq = sig("y_done", PAIR), sig("y_skip", PAIR), sig("y_gated", PAIR), sig("ysq", PAIR)
        lg_g, rsg_done = sig("lg_g", 1), sig("rsg_done", 1)
        y_turned, yT_ready = sig("y_turned", PAIR), sig("yT_ready", PAIR)
        mout_done, h_ready = sig("mout_done", 1), sig("h_ready", 1)

        c_loaded = sig("c_loaded", 16)
        k1_proj, k1_ready, v1_proj, v1_ready = sig("k1_proj", 1), sig("k1_ready", 1), sig("v1_proj", 1), sig("v1_ready", 1)
        hres_ready, st3_done, mv3_done = sig("hres_ready", 1), sig("st3_done", 1), sig("mv3_done", 1)
        lg3, rs3_done, xh3_ready = sig("lg3", 1), sig("rs3_done", 1), sig("xh3_ready", 1)
        xh3_turned, xh3T_hi, xh3T_ready = sig("xh3_turned", 1), sig("xh3T_hi", 1), sig("xh3T_ready", 1)
        q1_proj, q1_ready = sig("q1_proj", 1), sig("q1_ready", 1)
        scored3, maxed3, taken3 = sig("scored3", UC), sig("maxed3", UC), sig("taken3", UC)
        less3, turned3, exp3 = sig("less3", UC), sig("turned3", UC), sig("exp3", UC)
        weighed3, recip3, co_ready = sig("weighed3", UC), sig("recip3", UC), sig("co_ready", UC)
        co_turned, coT_hi, coT_ready, out_proj = sig("co_turned", 1), sig("coT_hi", 1), sig("coT_ready", 1), sig("out_proj", 1)
        out_ready, stored = sig("out_ready", 1), sig("stored", 16)

        block = ctx.enter_context(nc.Block())

        def run(engine, body, set_up_rest):
            def active(i):
                return [0 <= i - lag < NP for lag in (0, 1, 2, 3, -1)]
            body(-1, active(-1))
            body(0, active(0), set_up_rest)
            for i in range(1, 4):
                body(i, active(i))
            with engine.Fori(4, NP - 1) as i:
                body(i, [True] * 5)
            for i in range(NP - 1, NP + 3):
                body(i, active(i))

        def flat(t):
            return t[:].rearrange("q c t -> q (c t)")

        def rows(ap, n):
            return ap.rearrange("(o n) -> o n", o=1).broadcast_to([P, n])

        raw_w1 = [zc[:].rearrange("q b n -> q (b n)"), ez[:].rearrange("q b n -> q (b n)")]
        raw_wo0, raw_wq1, raw_wo1 = (t.rearrange("q (c d) -> q c d", c=KC) for t in (dtx[:, 0, :], dtx[:, 1, :], y[:, 0, :]))
        raw_b2 = y[:, 1, 0:D]
        LOADS_A = [
            (wk0[:], a["wk0"]), (wv0[:], a["wv0"]), (bk0[:], a["bk0"]), (bv_r[:], rows(a["bv0"], D)),
            (gam[:], rows(a["gammas"], H0)), (half16[:], a["half16"]), (tri[:], a["tri"]), (later[:], a["later"]),
            (ident[:], a["ident"]), (dist[:], a["dist"]),
        ]
        LOADS = [
            (raw_wo0, a["wo0"]), (raw_w1[0], a["w1"][:, 0, :]), (raw_w1[1], a["w1"][:, 1, :]),
            (b1[:], a["b1"]), (ln1w_c[:], a["ln1_w"]), (ln1b_c[:], a["ln1_b"]),
            (bo_r[:], rows(a["bo0"], D)), (raw_b2, rows(a["b2"], D)),
            (ln1w_r[:], rows(a["ln1_w_row"], D)), (ln1b_r[:], rows(a["ln1_b_row"], D)),
            (ln2w_r[:], rows(a["ln2_w_row"], D)), (ln2b_r[:], rows(a["ln2_b_row"], D)), (w2[:], a["w2"]),
            (win[:], a["win"]), (nw_c[:], a["m_norm_w"]), (wout[:], a["wout"]), (gw_c[:], a["gnorm_w"]),
            (selp[:], a["sel"]), (convw[:], a["conv_w"]), (convb[:], a["conv_b"]),
            (dtb[:], a["dt_bias"]), (nega[:], a["A_log"]), (eye4[:], a["eye4"]), (dskip_r[:], rows(a["D_skip"], HM)),
            (mask8[:], rows(a["mask"], P)), (half32[:], a["half32"]),
            (lw_c[:], a["ca_ln_w"]), (lb_c[:], a["ca_ln_b"]), (raw_wq1, a["wq1"]),
            (wk1[:], a["wk1"]), (wv1[:], a["wv1"]), (raw_wo1, a["wo1"]),
        ]
        A_LOADED, ALL_LOADED = 16 * len(LOADS_A), 16 * len(LOADS)

        @block.sync
        def _(sp_):
            eng = sp_
            xT_d = a["xT"].rearrange("(c q) t -> q c t", q=P)
            cT_d = a["cT"].rearrange("(c q) t -> q c t", q=P)
            x_d = a["x"]

            def load_a(p):
                eng.dma_start(xT[:], xT_d[:, :, bass.ts(p, T2)]).then_inc(a_loaded.sem, 16)
                eng.dma_start(cT[:], cT_d[:, :, bass.ts(p, T2)]).then_inc(a_loaded.sem, 16)

            def body(i, act_a, act_x, act_c, act_out):
                if act_a:
                    eng.wait_ge(v_proj.sem, v_proj.at(i, 1))
                    load_a(i + 1)
                if act_x:
                    eng.wait_ge(xb_ready.sem, xb_ready.at(i - 1, 1))
                    eng.dma_start(xin[:], x_d[:, bass.ts(i, PAIR), :]).then_inc(x_loaded.sem, 16)
                if act_c:
                    eng.wait_ge(v1_proj.sem, v1_proj.at(i - 3, 1))
                    eng.dma_start(cTc[:], cT_d[:, :, bass.ts(i - 2, T2)]).then_inc(c_loaded.sem, 16)
                if act_out:
                    eng.wait_ge(out_ready.sem, out_ready.at(i - 3, 1))
                    eng.dma_start(out[:, bass.ts(i - 3, PAIR), :], res[:]).then_inc(stored.sem, 16)

            load_a(0)
            for dst, src in LOADS_A:
                eng.dma_start(dst, src).then_inc(loaded_a.sem, 16)
            for dst, src in LOADS:
                eng.dma_start(dst, src).then_inc(loaded.sem, 16)

            def flags(i):
                return i + 1 < NP, i < NP, 0 <= i - 2 < NP, 0 <= i - 3 < NP
            for i in range(3):
                body(i, *flags(i))
            with eng.Fori(3, NP - 1) as i:
                body(i, True, True, True, True)
            for i in range(NP - 1, NP + 3):
                body(i, *flags(i))
            eng.wait_ge(stored.sem, 16 * NP)

        @block.gpsimd
        def _(pool):
            V = nc.gpsimd

            V.memset(v0[:], 1.0)
            V.memset(v1[:], 1.0)
            V.memset(cin[:], 0.0)
            V.memset(decay[:], 0.0)
            V.memset(wdt[:], 0.0)
            V.memset(eps_c[:], EPS)
            V.memset(tiny_c[:], TINY).then_inc(set_up.sem, 1)
            pool.wait_ge(set_up.sem, SETUP_A)

            def see_set_up():
                pool.wait_ge(loaded.sem, ALL_LOADED)
                pool.wait_ge(set_up.sem, SETUP_DONE)

            def less(out_, in_, m, done):
                V.tensor_tensor(out_.rearrange("q (n k) -> q n k", n=4), in_.rearrange("q (n k) -> q n k", n=4),
                                m.unsqueeze(2).broadcast_to([P, 4, P]), ALU.subtract).then_inc(done.sem, 1)

            def attention_normed(pos, p):
                u = pos // 2 - 1
                if pos % 2 == 1 and 0 <= u < UA:
                    pool.wait_ge(distanced.sem, distanced.at(p, u + 1))
                    d = dec0[:, u % 2, :].rearrange("q (n k) -> q n k", n=4)
                    V.tensor_tensor(d, d, rz[:, u % 2, :].unsqueeze(2).broadcast_to([P, 4, P]),
                                    ALU.mult).then_inc(normed.sem, 1)

            def attention_less(pos, p):
                s = pos // 2
                if pos % 2 == 0 and s < UA:
                    pool.wait_ge(maxed.sem, maxed.at(p, s + 1))
                    pool.wait_ge(turned1.sem, turned1.at(p, s - 1))
                    less(sm0[:, s % 2, :], sc0[:, s % 4, :], m1[:, s % 2, :], less1)
                u = s - 2
                if pos % 2 == 1 and 0 <= u < UA:
                    pool.wait_ge(maxed2.sem, maxed2.at(p, u + 1))
                    less(dec0[:, u % 2, :], dec0[:, u % 2, :], m2[:, u % 2, :], less2)

            def ffn_stage(pos, p):
                if pos == 0:
                    pool.wait_ge(x_loaded.sem, x_loaded.at(p, 16))
                    pool.wait_ge(s1_done.sem, s1_done.at(p - 1, 1))
                    V.tensor_tensor(xb[:], xin[:], bo_r[:].unsqueeze(1).broadcast_to([P, PAIR, D]),
                                    ALU.add).then_inc(xb_ready.sem, 1)
                if pos == 4:
                    pool.wait_ge(xh1_ready.sem, xh1_ready.at(p, 1))
                    V.tensor_tensor(x1b[:], s1[:], ln1w_r[:].unsqueeze(1).broadcast_to([P, PAIR, D]),
                                    ALU.mult).then_inc(x1m_done.sem, 1)
                    pool.wait_ge(x1m_done.sem, x1m_done.at(p, 1))
                    V.tensor_tensor(x1b[:], x1b[:], ln1b_r[:].unsqueeze(1).broadcast_to([P, PAIR, D]),
                                    ALU.add).then_inc(x1b_ready.sem, 1)
                if pos == 16:
                    pool.wait_ge(xh2_ready.sem, xh2_ready.at(p, 1))
                    pool.wait_ge(resid_ready.sem, resid_ready.at(p - 1, 1))
                    V.tensor_tensor(x2[:], s1[:], ln2w_r[:].unsqueeze(1).broadcast_to([P, PAIR, D]),
                                    ALU.mult).then_inc(x2m_done.sem, 1)
                    pool.wait_ge(x2m_done.sem, x2m_done.at(p, 1))
                    V.tensor_tensor(x2[:], x2[:], ln2b_r[:].unsqueeze(1).broadcast_to([P, PAIR, D]),
                                    ALU.add).then_inc(x2_ready.sem, 1)

            def mamba_stage(pos, p):
                if pos in (10, 11):
                    b = pos - 10
                    pool.wait_ge(z_sig.sem, z_sig.at(p, b + 1))
                    V.tensor_tensor(zs[:, b, :], zc[:, b, :], ez[:, b, :], ALU.mult).then_inc(zs_ready.sem, 1)

            def cross_stage(pos, p):
                v, r = divmod(pos - 6, 3)
                if pos >= 6 and r == 0 and v < UC:
                    pool.wait_ge(maxed3.sem, maxed3.at(p, v + 1))
                    less(sc3[:, 0, :], sc3[:, 0, :], m3[:, v % 2, :], less3)

            def body(i, on, set_up_rest={}):
                for pos in range(POS):
                    if pos in set_up_rest:
                        set_up_rest[pos]()
                    if on[1]:
                        ffn_stage(pos, i - 1)
                    if on[0]:
                        attention_normed(pos, i)
                    if on[2]:
                        mamba_stage(pos, i - 2)
                    if on[0]:
                        attention_less(pos, i)
                    if on[3]:
                        cross_stage(pos, i - 3)
            run(pool, body, {POS - 1: see_set_up})

        @block.scalar
        def _(act):
            S = nc.scalar
            act.preload_act_table_set("natural_log_exp_and_others")
            act.wait_ge(loaded_a.sem, A_LOADED)
            act.wait_ge(set_up.sem, 1)
            S.activation(gabs[:], gam[:], ACT.Abs).then_inc(set_up.sem, 1)
            act.wait_ge(set_up.sem, 2)
            S.activation(gabs[:], gabs[:], ACT.Exp, scale=-1.0).then_inc(set_up.sem, 1)
            act.wait_ge(set_up.sem, 3)
            S.activation(gabs[:], gabs[:], ACT.Ln, bias=1.0).then_inc(set_up.sem, 1)
            act.wait_ge(set_up.sem, SETUP_A)

            def set_up_decay():
                act.wait_ge(loaded.sem, ALL_LOADED)
                S.activation(nega[:], nega[:], ACT.Exp).then_inc(set_up.sem, 1)

            def see_set_up():
                act.wait_ge(set_up.sem, SETUP_DONE)

            def rsqrt(v_in, v_out, scale, done_log, done, p):
                S.activation(v_out, v_in, ACT.Ln, bias=eps_c[:], scale=scale).then_inc(done_log.sem, 1)
                act.wait_ge(done_log.sem, done_log.at(p, 1))
                S.activation(v_out, v_out, ACT.Exp, scale=-0.5).then_inc(done.sem, 1)

            def queries(pos, p):
                if pos == QPOS:
                    act.wait_ge(q_proj.sem, q_proj.at(p, 1))
                    for c in range(KC):
                        for par in range(2):
                            last = S.activation(q0[:, c, par, :], scores[:, c * T2:(c + 1) * T2], ACT.Identity,
                                                bias=qb0[:, c, par:par + 1], scale=half16[:, par:par + 1])
                    last.then_inc(q_ready.sem, 1)

            def attention(pos, p):
                u = pos // 2 - 2
                if pos % 2 == 0 and 0 <= u < UA:
                    act.wait_ge(normed.sem, normed.at(p, u + 1))
                    S.activation(dec0[:, u % 2, :], dec0[:, u % 2, :], ACT.Ln, bias=tiny_c[:]).then_inc(log_d.sem, 1)

            def attention_root(pos, p):
                u = pos // 2 - 2
                if pos % 2 == 0 and 0 <= u < UA:
                    act.wait_ge(log_d.sem, log_d.at(p, u + 1))
                    S.activation(dec0[:, u % 2, :], dec0[:, u % 2, :], ACT.Exp, scale=0.5).then_inc(root_d.sem, 1)

            def attention_weights(pos, p):
                s = pos // 2
                u = s - 2
                if pos % 2 == 0 and 0 <= u < UA:
                    act.wait_ge(root_d.sem, root_d.at(p, u + 1))
                    S.activation(dec0[:, u % 2, :], dec0[:, u % 2, :], ACT.Exp, scale=-1.0).then_inc(effect.sem, 1)
                u = s - 3
                if pos % 2 == 0 and 0 <= u < UA:
                    act.wait_ge(turned2.sem, turned2.at(p, u + 1))
                    S.activation(e1[:, u % 2, :], turned[:], ACT.Exp).then_inc(exp2.sem, 1)
                if pos % 2 == 1 and s < UA:
                    act.wait_ge(turned1.sem, turned1.at(p, s + 1))
                    act.wait_ge(summed.sem, summed.at(p, s - 1))
                    S.activation(e0[:, s % 2, :], turned[:], ACT.Exp).then_inc(exp1.sem, 1)

            def ffn_stage(pos, p):
                if pos == 0:
                    act.wait_ge(att_turned.sem, att_turned.at(p, 1))
                    S.activation(flat(bT[0]), ffn[:], ACT.Copy).then_inc(attT_hi.sem, 1)
                if pos == 2:
                    act.wait_ge(mv1_done.sem, mv1_done.at(p, 1))
                    rsqrt(mv1[:, :, 1], rs1[:], 1.0, lg1, rs1_done, p)
                if pos == 3:
                    act.wait_ge(x1_turned.sem, x1_turned.at(p, 1))
                    S.activation(flat(bT[0]), ffn[:], ACT.Copy).then_inc(x1T_hi.sem, 1)
                if pos in (5, 7):
                    n = pos - 5
                    act.wait_ge(up_done.sem, up_done.at(p, n + 1))
                    for c in range(2):
                        last = S.activation(hT[:, 2 * n + c, :], ffn[:, c * T2:(c + 1) * T2], ACT.Relu,
                                            bias=b1[:, 2 * n + c:2 * n + c + 1])
                    last.then_inc(relu_a.sem, 1)
                if pos == 12:
                    act.wait_ge(mv2_done.sem, mv2_done.at(p, 1))
                    rsqrt(mv2[:, :, 1], rs2[:], 1.0, lg2, rs2_done, p)
                if pos == 17:
                    act.wait_ge(x2_ready.sem, x2_ready.at(p, 1))
                    for b in range(PAIR):
                        if b:
                            act.wait_ge(sq_done.sem, sq_done.at(p, b))
                        S.activation(x1b[:, b, :], x2[:, b, :], ACT.Square,
                                     accum_out=ms[:, b:b + 1]).then_inc(sq_done.sem, 1)
                    act.wait_ge(sq_done.sem, sq_done.at(p, PAIR))
                    rsqrt(ms[:], ms[:], 1.0 / D, lg_r, rsr_done, p)
                if pos == 19:
                    act.wait_ge(xn_turned.sem, xn_turned.at(p, 1))
                    S.activation(flat(xnT), ffn[:], ACT.Copy).then_inc(xnT_ready.sem, 1)

            def mamba_stage(pos, p):
                if pos == 3:
                    act.wait_ge(dt_raw.sem, dt_raw.at(p, 1))
                    S.activation(dta[:], dtv[:], ACT.Abs).then_inc(dt_abs.sem, 1)
                if pos == 5:
                    act.wait_ge(dt_abs.sem, dt_abs.at(p, 1))
                    S.activation(dta[:], dta[:], ACT.Exp, scale=-1.0).then_inc(dt_exp.sem, 1)
                if pos < 3:
                    lo, hi = CHUNKS[pos]
                    act.wait_ge(xbc_done.sem, xbc_done.at(p, pos + 1))
                    act.wait_ge(xc_ready.sem, xc_ready.at(p - 1, 3))
                    for n, m in enumerate(range(lo, hi)):
                        S.activation(acc[:, m, :], mamba[pos % 2][:, n * T2:(n + 1) * T2], ACT.Identity,
                                     bias=convb[:, m:m + 1], scale=convw[:, m, TAPS - 1:TAPS])
                    S.activation(esig[:, 2 * lo:2 * hi, :],
                                 mamba[pos % 2][:].rearrange("q (m t) -> q m t", t=P),
                                 ACT.Copy).then_inc(conv_in.sem, 1)
                if 2 <= pos < 5:
                    lo, hi = CHUNKS[pos - 2]
                    act.wait_ge(tap_done.sem, tap_done.at(p, 6 * (pos - 1)))
                    S.activation(esig[:, 2 * lo:2 * hi, :], acc_v[:, 2 * lo:2 * hi, :], ACT.Exp, scale=-1.0).then_inc(esig_done.sem, 1)
                if pos == 5:
                    act.wait_ge(dt_exp.sem, dt_exp.at(p, 1))
                    S.activation(dta[:], dta[:], ACT.Ln, bias=1.0).then_inc(dt_log.sem, 1)
                if pos in (4, 5):
                    b = pos - 4
                    act.wait_ge(z_done.sem, z_done.at(p, b + 1))
                    act.wait_ge(y_gated.sem, y_gated.at(p - 1, PAIR))
                    S.activation(zc[:, b, :], mamba[pos % 2][:], ACT.Copy)
                    S.activation(ez[:, b, :], mamba[pos % 2][:], ACT.Exp, scale=-1.0).then_inc(z_exp.sem, 1)
                if 4 <= pos < 7:
                    lo, hi = CHUNKS[pos - 4]
                    act.wait_ge(eclip.sem, eclip.at(p, pos - 3))
                    S.activation(esig[:, 2 * lo:2 * hi, :], esig[:, 2 * lo:2 * hi, :], ACT.Ln, bias=1.0).then_inc(lnsig.sem, 1)
                if pos == 6:
                    act.wait_ge(sp_ready.sem, sp_ready.at(p, 1))
                    S.activation(decay[:, :, 1:P], sp[:].rearrange("q (b t) -> q b t", b=PAIR)[:, :, 1:P], ACT.Exp,
                                 scale=nega[:]).then_inc(decay_ready.sem, 1)
                if pos in (10, 11):
                    b = pos - 10
                    act.wait_ge(z_clip.sem, z_clip.at(p, b + 1))
                    S.activation(ez[:, b, :], ez[:, b, :], ACT.Ln, bias=1.0).then_inc(z_log.sem, 1)
                if 4 <= pos < 7:
                    lo, hi = CHUNKS[pos - 4]
                    act.wait_ge(lnsig.sem, lnsig.at(p, pos - 3))
                    S.activation(esig[:, 2 * lo:2 * hi, :], esig[:, 2 * lo:2 * hi, :], ACT.Exp, scale=-1.0).then_inc(sigm.sem, 1)
                if pos in (10, 11):
                    b = pos - 10
                    act.wait_ge(z_log.sem, z_log.at(p, b + 1))
                    S.activation(ez[:, b, :], ez[:, b, :], ACT.Exp, scale=-1.0).then_inc(z_sig.sem, 1)
                if pos == 11:
                    act.wait_ge(cb_done.sem, cb_done.at(p, 1))
                    S.activation(cbdt[:], mamba[0][:, 0:2 * P + PAIR * HM], ACT.Copy).then_inc(cb_ready.sem, 1)
                if pos in (16, 17):
                    b = pos - 16
                    act.wait_ge(y_gated.sem, y_gated.at(p, b + 1))
                    act.wait_ge(ysq.sem, ysq.at(p, b))
                    S.activation(sqy[:], y[:, b, :], ACT.Square, accum_out=ssq[:, b:b + 1]).then_inc(ysq.sem, 1)
                if pos in (19, 20):
                    b = pos - 19
                    act.wait_ge(y_turned.sem, y_turned.at(p, b + 1))
                    S.activation(yT[:, b, :], mamba[(b + 1) % 2][:], ACT.Copy).then_inc(yT_ready.sem, 1)
                if pos == 19:
                    act.wait_ge(ysq.sem, ysq.at(p, PAIR))
                    rsqrt(ssq[:], ssq[:], 1.0 / DI, lg_g, rsg_done, p)

            def cross_stage(pos, p):
                if pos == 0:
                    act.wait_ge(k1_proj.sem, k1_proj.at(p, 1))
                    S.activation(k1[:].rearrange("q c t -> q (c t)"), cross[:], ACT.Copy).then_inc(k1_ready.sem, 1)
                if pos == 0:
                    act.wait_ge(v1_proj.sem, v1_proj.at(p, 1))
                    S.activation(v1[:, :, :, 0:DH1], cross[:].rearrange("q (b n d) -> q b n d", b=PAIR, d=DH1),
                                 ACT.Copy).then_inc(v1_ready.sem, 1)
                    act.wait_ge(mv3_done.sem, mv3_done.at(p, 1))
                    rsqrt(mv3[:, :, 1], rs3[:], 1.0, lg3, rs3_done, p)
                v, r = divmod(pos - 6, 3)
                if pos >= 6 and r == 2 and v < UC:
                    act.wait_ge(turned3.sem, turned3.at(p, v + 1))
                    S.activation(e3[:, 0, :], cross[:], ACT.Exp).then_inc(exp3.sem, 1)
                if pos == 3:
                    act.wait_ge(xh3_turned.sem, xh3_turned.at(p, 1))
                    S.activation(flat(hT1[0]), cross[:], ACT.Copy).then_inc(xh3T_hi.sem, 1)
                if pos == 4:
                    act.wait_ge(q1_proj.sem, q1_proj.at(p, 1))
                    for c in range(KC):
                        for par in range(2):
                            last = S.activation(q1[:, c, par, :], cross[:, c * T2:(c + 1) * T2], ACT.Identity,
                                                bias=qb1[:, c, par:par + 1], scale=half32[:, par:par + 1])
                    last.then_inc(q1_ready.sem, 1)
                if pos == 20:
                    act.wait_ge(co_turned.sem, co_turned.at(p, 1))
                    S.activation(flat(hT1[0]), cross[:], ACT.Copy).then_inc(coT_hi.sem, 1)

            def body(i, on, set_up_rest={}):
                for pos in range(POS):
                    if pos in set_up_rest:
                        set_up_rest[pos]()
                    if on[0]:
                        attention(pos, i)
                    if on[1]:
                        ffn_stage(pos, i - 1)
                    if on[0]:
                        attention_root(pos, i)
                    if on[2]:
                        mamba_stage(pos, i - 2)
                    if on[0]:
                        attention_weights(pos, i)
                    if on[3]:
                        cross_stage(pos, i - 3)
                    if on[4]:
                        queries(pos, i + 1)
            run(act, body, {6: set_up_decay, POS - 1: see_set_up})

        @block.vector
        def _(dve):
            V = nc.vector
            dve.wait_ge(loaded_a.sem, A_LOADED)
            dve.wait_ge(set_up.sem, 4)
            n = [4]

            def step(ins):
                n[0] += 1
                ins.then_inc(set_up.sem, 1)
                dve.wait_ge(set_up.sem, n[0])

            def parts(to, at_, raw, width):
                step(V.tensor_copy(to[0][:, at_, 0:width], raw))
                step(V.tensor_tensor(to[1][:, at_, 0:width], raw, to[0][:, at_, 0:width].bitcast(F32), ALU.subtract))

            step(V.tensor_scalar(gam[:], gam[:], 0.0, None, ALU.max))
            step(V.tensor_tensor(gam[:], gam[:], gabs[:], ALU.add))
            step(V.tensor_tensor(gam2[:], gam[:], gam[:], ALU.mult))
            for c in range(KC):
                for par in range(2):
                    step(V.tensor_tensor(qb0[:, c, par:par + 1], bk0[:, c:c + 1], half16[:, par:par + 1], ALU.mult))
            assert n[0] == SETUP_A, n

            def set_up_inputs():
                dve.wait_ge(loaded.sem, ALL_LOADED)
                n[0] += 1
                dve.wait_ge(set_up.sem, n[0])
                step(V.tensor_copy(sel[:], selp[:]))
                step(V.tensor_scalar(nega[:], nega[:], -1.0, None, ALU.mult))
                step(V.tensor_copy(padmask[:], mask8[:]))
                step(V.tensor_scalar(padmask[:], padmask[:], -1e30, None, ALU.mult))
                step(V.tensor_tensor(ln1b_r[:], ln1b_r[:], raw_b2, ALU.add))
                for c in range(KC):
                    step(V.tensor_scalar(win[:, c, :], win[:, c, :], nw_c[:, c:c + 1], None, ALU.mult))
                    for r0 in (0, 32):
                        step(V.tensor_copy(wdt[:, c, r0:r0 + HM], win[:, c, NIN - HM:NIN]))

            def set_up_outputs():
                for c in range(KC):
                    parts(wo0, c, raw_wo0[:, c, :], D)
                    parts(wo1, c, raw_wo1[:, c, :], D)
                for c in range(DI // P):
                    step(V.tensor_scalar(wout[:, c, :], wout[:, c, :], gw_c[:, c:c + 1], None, ALU.mult))

            def set_up_normed(c):
                if c == 0:
                    set_up_biases()
                step(V.tensor_scalar(raw_wq1[:, c, :], raw_wq1[:, c, :], lw_c[:, c:c + 1], None, ALU.mult))
                parts(wq1, c, raw_wq1[:, c, :], D)
                step(V.tensor_scalar(raw_w1[c], raw_w1[c], ln1w_c[:, c:c + 1], None, ALU.mult))
                parts(w1, c, raw_w1[c], F)

            def set_up_biases():
                n[0] += 1
                dve.wait_ge(set_up.sem, n[0])
                for c in range(KC):
                    for par in range(2):
                        step(V.tensor_tensor(qb1[:, c, par:par + 1], cross[:, c:c + 1], half32[:, par:par + 1], ALU.mult))
                step(V.tensor_tensor(b1[:], b1[:], cross[:, KC:KC + FM], ALU.add))

            def moments(x_, st, mv, st_sig, mv_sig, p):
                for b in range(PAIR):
                    last = V.bn_stats(st[:, b, :], x_[:, b, :])
                last.then_inc(st_sig.sem, 1)
                dve.wait_ge(loaded.sem, ALL_LOADED)
                dve.wait_ge(st_sig.sem, st_sig.at(p, 1))
                for b in range(PAIR):
                    last = V.bn_aggr(mv[:, b, :], st[:, b, :])
                last.then_inc(mv_sig.sem, 1)

            def centre(o, x_, mv, rs, done):
                for b in range(PAIR):
                    last = V.tensor_scalar(o[:, b, :], x_[:, b, :], mv[:, b, 0:1], rs[:, b:b + 1],
                                           ALU.subtract, ALU.mult)
                last.then_inc(done.sem, 1)

            def heads(ap):
                return ap.rearrange("q (n k) -> q n k", n=4)

            def keys(pos, p):
                if pos == QPOS + 2:
                    dve.wait_ge(k_proj.sem, k_proj.at(p, 1))
                    for c in range(KC):
                        last = V.tensor_scalar(k0[:, c, :], scores[:, c * T2:(c + 1) * T2], bk0[:, c:c + 1], None, ALU.add)
                    last.then_inc(k_ready.sem, 1)

            def attention(pos, p):
                s = pos // 2
                if pos == 0:
                    dve.wait_ge(v_proj.sem, v_proj.at(p, 1))
                    V.tensor_tensor(v0[:, :, :, 0:DH0], sums[:].rearrange("q (b n d) -> q b n d", b=PAIR, d=DH0),
                                    bv_r[:].rearrange("q (n d) -> q n d", d=DH0).unsqueeze(1).broadcast_to([P, PAIR, H0, DH0]),
                                    ALU.add).then_inc(v_ready.sem, 1)
                u = s - 1
                if pos % 2 == 1 and 0 <= u < UA:
                    dve.wait_ge(summed.sem, summed.at(p, u + 1))
                    dve.wait_ge(normed.sem, normed.at(p, u - 1))
                    dve.wait_ge(turned2.sem, turned2.at(p, u - 1))
                    V.reciprocal(rz[:, u % 2, :], heads(sums[:])[:, :, P - 1]).then_inc(recip1.sem, 1)
                    dve.wait_ge(recip1.sem, recip1.at(p, 2 * u + 1))
                    rzu = rz[:, u % 2, :].rearrange("q (c e) -> q c e", c=2)
                    V.tensor_tensor(rzu, rzu, gam2[:].rearrange("q (c j e) -> q j c e", c=2, j=4)[:, u % 4, :, :],
                                    ALU.mult).then_inc(recip1.sem, 1)
                    V.scalar_tensor_tensor(heads(dec0[:, u % 2, :]), heads(sums[:]), 0.0,
                                           dist[:].unsqueeze(1).broadcast_to([P, 4, P]),
                                           ALU.max, ALU.mult).then_inc(distanced.sem, 1)

            def attention_max(pos, p):
                s = pos // 2
                if pos % 2 == 0 and s < UA:
                    dve.wait_ge(scored.sem, scored.at(p, s + 1))
                    dve.wait_ge(decayed.sem, decayed.at(p, s - 3))
                    dve.wait_ge(less1.sem, less1.at(p, s - 3))
                    V.tensor_tensor(heads(sc0[:, s % 4, :]), heads(scores[:]), later[:].unsqueeze(1).broadcast_to([P, 4, P]),
                                    ALU.add).then_inc(taken.sem, 1)
                    dve.wait_ge(taken.sem, taken.at(p, s + 1))
                    dve.wait_ge(less1.sem, less1.at(p, s - 1))
                    V.tensor_reduce(m1[:, s % 2, :], heads(sc0[:, s % 4, :]), AX, ALU.max).then_inc(maxed.sem, 1)

            def attention_decayed(pos, p):
                u = pos // 2 - 2
                if pos % 2 == 1 and 0 <= u < UA:
                    dve.wait_ge(effect.sem, effect.at(p, u + 1))
                    V.scalar_tensor_tensor(dec0[:, u % 2, :], dec0[:, u % 2, :], 1e-5, sc0[:, u % 4, :],
                                           ALU.max, ALU.mult).then_inc(decayed.sem, 1)
                    dve.wait_ge(decayed.sem, decayed.at(p, u + 1))
                    dve.wait_ge(less2.sem, less2.at(p, u - 1))
                    V.tensor_reduce(m2[:, u % 2, :], heads(dec0[:, u % 2, :]), AX, ALU.max).then_inc(maxed2.sem, 1)

            def attention_out(pos, p):
                u = pos // 2 - 3
                if pos % 2 == 1 and 0 <= u < UA and u % 4 == 3:
                    b = u // 4
                    o = attn_out[:, 0:H0 * (DH0 + 1)].rearrange("q (n d) -> q n d", d=DH0 + 1)
                    dve.wait_ge(weighed.sem, weighed.at(p, u + 1))
                    V.reciprocal(rz2[:], o[:, :, DH0]).then_inc(recip2.sem, 1)
                    dve.wait_ge(recip2.sem, recip2.at(p, b + 1))
                    dve.wait_ge(att_turned.sem, att_turned.at(p - 1, 1))
                    V.tensor_tensor(att[:, b, :].rearrange("q (n d) -> q n d", d=DH0), o[:, :, 0:DH0],
                                    rz2[:].unsqueeze(2).broadcast_to([P, H0, DH0]), ALU.mult).then_inc(att_ready.sem, 1)

            def ffn_stage(pos, p):
                if pos == 4:
                    dve.wait_ge(x1T_hi.sem, x1T_hi.at(p, 1))
                    V.tensor_tensor(flat(bT[1]), ffn[:], flat(bT[0]).bitcast(F32), ALU.subtract).then_inc(x1T_ready.sem, 1)
                if pos == 0:
                    dve.wait_ge(attT_hi.sem, attT_hi.at(p, 1))
                    V.tensor_tensor(flat(bT[1]), ffn[:], flat(bT[0]).bitcast(F32), ALU.subtract).then_inc(attT_ready.sem, 1)
                if pos == 2:
                    dve.wait_ge(wo_done.sem, wo_done.at(p, 1))
                    dve.wait_ge(xb_ready.sem, xb_ready.at(p, 1))
                    V.tensor_tensor(s1[:].rearrange("q b d -> q (b d)"), ffn[:], xb[:].rearrange("q b d -> q (b d)"),
                                    ALU.add).then_inc(s1_done.sem, 1)
                    dve.wait_ge(s1_done.sem, s1_done.at(p, 1))
                    moments(s1, st1, mv1, st1_done, mv1_done, p)
                if pos in (6, 8):
                    n_ = pos - 5
                    dve.wait_ge(up_done.sem, up_done.at(p, n_ + 1))
                    for c in range(2):
                        m = 2 * n_ + c
                        last = V.tensor_scalar(hT[:, m, :], ffn[:, c * T2:(c + 1) * T2], b1[:, m:m + 1], 0.0,
                                               ALU.add, ALU.max)
                    last.then_inc(relu_v.sem, 1)
                if pos == 12:
                    dve.wait_ge(down_done.sem, down_done.at(p, 1))
                    dve.wait_ge(x1b_ready.sem, x1b_ready.at(p, 1))
                    V.tensor_tensor(s1[:].rearrange("q b d -> q (b d)"), ffn[:], x1b[:].rearrange("q b d -> q (b d)"),
                                    ALU.add).then_inc(s2_done.sem, 1)
                    dve.wait_ge(s2_done.sem, s2_done.at(p, 1))
                    moments(s1, st2, mv2, st2_done, mv2_done, p)
                if pos == 3:
                    dve.wait_ge(rs1_done.sem, rs1_done.at(p, 1))
                    dve.wait_ge(x1b_ready.sem, x1b_ready.at(p - 1, 1))
                    centre(s1, s1, mv1, rs1, xh1_ready)
                if pos == 14:
                    dve.wait_ge(rs2_done.sem, rs2_done.at(p, 1))
                    dve.wait_ge(x2_ready.sem, x2_ready.at(p - 1, 1))
                    centre(s1, s1, mv2, rs2, xh2_ready)
                if pos == 18:
                    dve.wait_ge(rsr_done.sem, rsr_done.at(p, 1))
                    for b in range(PAIR):
                        last = V.tensor_scalar(s1[:, b, :], x2[:, b, :], ms[:, b:b + 1], None, ALU.mult)
                    last.then_inc(xn_ready.sem, 1)

            def mamba_stage(pos, p):
                if pos == 0:
                    dve.wait_ge(x2_ready.sem, x2_ready.at(p, 1))
                    dve.wait_ge(h_ready.sem, h_ready.at(p - 1, 1))
                    V.tensor_copy(resid[:], x2[:]).then_inc(resid_ready.sem, 1)
                if pos == 3:
                    dve.wait_ge(dt_done.sem, dt_done.at(p, 1))
                    V.tensor_scalar(dtv[:], mamba[1][0:DTR, 0:T2], dtb[:], None, ALU.add).then_inc(dt_raw.sem, 1)
                    dve.wait_ge(dt_raw.sem, dt_raw.at(p, 1))
                    V.tensor_scalar(dtp[:], dtv[:], 0.0, None, ALU.max).then_inc(dt_pos.sem, 1)
                if 1 <= pos < 4:
                    c = pos - 1
                    dve.wait_ge(conv_in.sem, conv_in.at(p, c + 1))
                    for k in range(TAPS - 1):
                        for n_, m in enumerate(range(*CHUNKS[c])):
                            if k:
                                dve.wait_ge(tap_done.sem, tap_done.at(p, 6 * c + 2 * k + n_ - 1))
                            o = acc[:, m, :].rearrange("q (b t) -> q b t", b=PAIR)
                            V.scalar_tensor_tensor(o, cin[:, m, :, k:k + P], convw[:, m, k:k + 1], o,
                                                   ALU.mult, ALU.add).then_inc(tap_done.sem, 1)
                if 3 <= pos < 6:
                    lo, hi = CHUNKS[pos - 3]
                    dve.wait_ge(esig_done.sem, esig_done.at(p, pos - 2))
                    V.tensor_scalar(esig[:, 2 * lo:2 * hi, :], esig[:, 2 * lo:2 * hi, :], SIG_MAX, None, ALU.min).then_inc(eclip.sem, 1)
                if pos == 6:
                    dve.wait_ge(dt_log.sem, dt_log.at(p, 1))
                    dve.wait_ge(dt_pos.sem, dt_pos.at(p, 1))
                    V.tensor_tensor(sp[:], dtp[:], dta[:], ALU.add).then_inc(sp_ready.sem, 1)
                if pos in (8, 9):
                    b = pos - 8
                    dve.wait_ge(z_exp.sem, z_exp.at(p, b + 1))
                    V.tensor_scalar(ez[:, b, :], ez[:, b, :], SIG_MAX, None, ALU.min).then_inc(z_clip.sem, 1)
                if 5 <= pos < 8:
                    lo, hi = CHUNKS[pos - 5]
                    dve.wait_ge(sigm.sem, sigm.at(p, pos - 4))
                    V.tensor_tensor(acc_v[:, 2 * lo:2 * hi, :], acc_v[:, 2 * lo:2 * hi, :], esig[:, 2 * lo:2 * hi, :], ALU.mult).then_inc(xc_ready.sem, 1)
                if pos == 6:
                    dve.wait_ge(decay_ready.sem, decay_ready.at(p, 1))
                    V.tensor_copy(decay_p[:], decay[:]).then_inc(decay_high.sem, 1)
                    dve.wait_ge(decay_high.sem, decay_high.at(p, 1))
                    V.tensor_tensor(decay_p[32:DTR], decay[32:DTR], decay_p[32:DTR].bitcast(F32),
                                    ALU.subtract).then_inc(decay_parts.sem, 1)
                if pos in (8, 9, 11, 12):
                    k = (8, 9, 11, 12).index(pos)
                    dve.wait_ge(spread.sem, spread.at(p, k + 1))
                    V.tensor_tensor_scan(g[:, k // 2, (k % 2) * 512:(k % 2 + 1) * 512], mamba[MB[pos]][:], eye4[:], 0.0,
                                         ALU.mult, ALU.add).then_inc(scanned.sem, 1)
                if pos in (11, 13):
                    b = (pos - 11) // 2
                    dve.wait_ge(scanned.sem, scanned.at(p, 2 * b + 2))
                    dve.wait_ge(cb_ready.sem, cb_ready.at(p, 1))
                    gb = g[:, b, :].rearrange("q (n t) -> q n t", t=P)
                    V.tensor_tensor(gb, gb, cbdt[:, b * P:(b + 1) * P].unsqueeze(1).broadcast_to([P, HM, P]),
                                    ALU.mult).then_inc(mixed.sem, 1)
                if pos in (14, 15):
                    b = pos - 14
                    dve.wait_ge(x_turned.sem, x_turned.at(p, b + 1))
                    xt = mamba[MB[pos]][:].rearrange("q (n d) -> q n d", d=HD)
                    V.tensor_tensor(dtx[:, b, :].rearrange("q (n d) -> q n d", d=HD), xt,
                                    cbdt[:, 2 * P + b * HM:2 * P + (b + 1) * HM].unsqueeze(2).broadcast_to([P, HM, HD]),
                                    ALU.mult)
                    V.tensor_tensor(y[:, b, :].rearrange("q (n d) -> q n d", d=HD), xt,
                                    dskip_r[:].unsqueeze(2).broadcast_to([P, HM, HD]), ALU.mult).then_inc(xtok.sem, 1)
                if pos in (16, 17):
                    b = pos - 16
                    dve.wait_ge(y_done.sem, y_done.at(p, b + 1))
                    V.tensor_tensor(y[:, b, :], mamba[MB[pos]][:], y[:, b, :], ALU.add).then_inc(y_skip.sem, 1)
                    dve.wait_ge(y_skip.sem, y_skip.at(p, b + 1))
                    dve.wait_ge(zs_ready.sem, zs_ready.at(p, b + 1))
                    V.tensor_tensor(y[:, b, :], y[:, b, :], zs[:, b, :], ALU.mult).then_inc(y_gated.sem, 1)
                if pos == 21:
                    dve.wait_ge(mout_done.sem, mout_done.at(p, 1))
                    dve.wait_ge(rsg_done.sem, rsg_done.at(p, 1))
                    for b in range(PAIR):
                        last = V.scalar_tensor_tensor(h[:, b, :], mamba[1][:, b * D:(b + 1) * D], ssq[:, b:b + 1],
                                                      resid[:, b, :], ALU.mult, ALU.add)
                    last.then_inc(h_ready.sem, 1)

            def cross_stage(pos, p):
                if pos == 3:
                    dve.wait_ge(xh3T_hi.sem, xh3T_hi.at(p, 1))
                    V.tensor_tensor(flat(hT1[1]), cross[:], flat(hT1[0]).bitcast(F32), ALU.subtract).then_inc(xh3T_ready.sem, 1)
                if pos == 20:
                    dve.wait_ge(coT_hi.sem, coT_hi.at(p, 1))
                    V.tensor_tensor(flat(hT1[1]), cross[:], flat(hT1[0]).bitcast(F32), ALU.subtract).then_inc(coT_ready.sem, 1)
                if pos == 2:
                    dve.wait_ge(rs3_done.sem, rs3_done.at(p, 1))
                    dve.wait_ge(hres_ready.sem, hres_ready.at(p, 1))
                    centre(h, h, mv3, rs3, xh3_ready)
                v, r = divmod(pos - 6, 3)
                if pos >= 6 and r == 0 and v < UC:
                    dve.wait_ge(scored3.sem, scored3.at(p, v + 1))
                    V.tensor_tensor(heads(sc3[:, 0, :]), heads(cross[:]), padmask[:].unsqueeze(1).broadcast_to([P, 4, P]),
                                    ALU.add).then_inc(taken3.sem, 1)
                    dve.wait_ge(taken3.sem, taken3.at(p, v + 1))
                    V.tensor_reduce(m3[:, v % 2, :], heads(sc3[:, 0, :]), AX, ALU.max).then_inc(maxed3.sem, 1)
                if pos == 0:
                    dve.wait_ge(h_ready.sem, h_ready.at(p, 1))
                    dve.wait_ge(out_ready.sem, out_ready.at(p - 1, 1))
                    V.tensor_copy(hres[:], h[:]).then_inc(hres_ready.sem, 1)
                    moments(h, st3, mv3, st3_done, mv3_done, p)
                v, r = divmod(pos - 10, 3)
                if pos >= 10 and r == 0 and v < UC:
                    b, jj = divmod(v, 2)
                    o = cross[:, 0:4 * (DH1 + 1)].rearrange("q (c e d) -> q c e d", c=2, e=2)
                    dve.wait_ge(weighed3.sem, weighed3.at(p, v + 1))
                    dve.wait_ge(co_ready.sem, co_ready.at(p, v))
                    dve.wait_ge(stored.sem, stored.at(p, 0))
                    V.reciprocal(rz3[:].rearrange("q (c e) -> q c e", c=2), o[:, :, :, DH1]).then_inc(recip3.sem, 1)
                    dve.wait_ge(recip3.sem, recip3.at(p, v + 1))
                    V.tensor_tensor(co[:, b, :].rearrange("q (c j e d) -> q j c e d", c=2, j=2, e=2)[:, jj, :, :, :],
                                    o[:, :, :, 0:DH1],
                                    rz3[:].rearrange("q (c e) -> q c e", c=2).unsqueeze(3).broadcast_to([P, 2, 2, DH1]),
                                    ALU.mult).then_inc(co_ready.sem, 1)
                if pos == 21:
                    dve.wait_ge(out_proj.sem, out_proj.at(p, 1))
                    V.tensor_tensor(res[:].rearrange("q b d -> q (b d)"), cross[:], hres[:].rearrange("q b d -> q (b d)"),
                                    ALU.add).then_inc(out_ready.sem, 1)

            def body(i, on, set_up_rest={}):
                for pos in range(POS):
                    if pos in set_up_rest:
                        set_up_rest[pos]()
                    if on[1]:
                        ffn_stage(pos, i - 1)
                    if on[0]:
                        attention(pos, i)
                    if on[0]:
                        attention_max(pos, i)
                        attention_decayed(pos, i)
                    if on[0]:
                        attention_out(pos, i)
                    if on[2]:
                        mamba_stage(pos, i - 2)
                    if on[4]:
                        keys(pos, i + 1)
                    if on[3]:
                        cross_stage(pos, i - 3)
            run(dve, body, {7: set_up_inputs, 10: set_up_outputs, 14: lambda: set_up_normed(0), 17: lambda: set_up_normed(1)})
            assert n[0] == SETUP_DONE, n

        @block.tensor
        def _(pe):
            M = nc.tensor
            pe.wait_ge(loaded_a.sem, A_LOADED)
            pe.wait_ge(set_up.sem, SETUP_A)

            def set_up_query_bias():
                pe.wait_ge(loaded.sem, ALL_LOADED)
                for c in range(KC):
                    for k in range(KC):
                        M.matmul(cross[:, c:c + 1], raw_wq1[:, k, c * P:(c + 1) * P], lb_c[:, k:k + 1],
                                 start=(k == 0), stop=(k == KC - 1))

            def set_up_ffn_bias(lo, hi):
                pe.wait_ge(set_up.sem, SETUP_TENSOR)
                for m in range(lo, hi):
                    for k in range(KC):
                        last = M.matmul(cross[:, KC + m:KC + m + 1], raw_w1[k][:, m * P:(m + 1) * P],
                                        ln1b_c[:, k:k + 1], start=(k == 0), stop=(k == KC - 1))
                if hi == FM:
                    last.then_inc(set_up.sem, 1)

            def see_set_up():
                pe.wait_ge(set_up.sem, SETUP_DONE)

            WHOLE, PARTS = [(0, 0)], [(0, 0), (0, 1), (1, 0)]

            def product(out_, terms):
                for n_, (w, x_) in enumerate(terms):
                    last = M.matmul(out_, w, x_, start=(n_ == 0), stop=(n_ == len(terms) - 1))
                return last

            def project(bank_, w, xt, parts=WHOLE):
                for c in range(KC):
                    last = product(bank_[:, c * T2:(c + 1) * T2],
                                   [(w[i_][:, k, c * P:(c + 1) * P], xt[j_][:, k, :])
                                    for k in range(KC) for i_, j_ in parts])
                return last

            def project_tokens(bank_, xt, w, parts=WHOLE, chunks=KC):
                for b in range(PAIR):
                    last = product(bank_[:, b * D:(b + 1) * D],
                                   [(xt(i_, k, b), w[j_][:, k, :]) for k in range(chunks) for i_, j_ in parts])
                return last

            def tokens(xt):
                return lambda i_, k, b: xt[i_][:, k, b * P:(b + 1) * P]

            def turn(bank_, src):
                for c in range(KC):
                    for b in range(PAIR):
                        last = M.transpose(bank_[:, c * T2 + b * P:c * T2 + (b + 1) * P],
                                           src[:, b, c * P:(c + 1) * P], ident[:])
                return last

            def turn_heads(bank_, src):
                for n_ in range(4):
                    last = M.transpose(bank_[:, n_ * P:(n_ + 1) * P], src[:, n_ * P:(n_ + 1) * P], ident[:])
                return last

            def score(bank_, q, k, r0, nrow, b):
                for c in range(KC):
                    for par in range(2):
                        n_ = 2 * c + par
                        last = M.matmul(bank_[:, n_ * P:(n_ + 1) * P], q[r0:r0 + nrow, c, par, b * P:(b + 1) * P],
                                        k[r0:r0 + nrow, c, b * P:(b + 1) * P], start=True, stop=True)
                return last

            def queries_keys(pos, p):
                if pos == QPOS:
                    pe.wait_ge(a_loaded.sem, a_loaded.at(p, 32))
                    pe.wait_ge(taken.sem, taken.at(p, 0))
                    project(scores, [wk0], [xT]).then_inc(q_proj.sem, 1)
                if pos == QPOS + 2:
                    pe.wait_ge(q_ready.sem, q_ready.at(p, 1))
                    project(scores, [wk0], [cT]).then_inc(k_proj.sem, 1)

            def attention_scores(pos, p):
                if pos == 0:
                    pe.wait_ge(k_ready.sem, k_ready.at(p, 1))
                    score_unit(0, p)
                    pe.wait_ge(distanced.sem, distanced.at(p, 0))
                    project_tokens(sums, tokens([cT]), [wv0]).then_inc(v_proj.sem, 1)
                elif pos % 2 == 0 and pos // 2 < UA:
                    score_unit(pos // 2, p)

            def score_unit(u, p):
                pe.wait_ge(taken.sem, taken.at(p, u))
                score(scores, q0, k0, 32 * (u % 4), 32, u // 4).then_inc(scored.sem, 1)

            def attention_turns(pos, p):
                s = pos // 2
                if pos % 2 == 1 and s < UA:
                    pe.wait_ge(less1.sem, less1.at(p, s + 1))
                    pe.wait_ge(exp1.sem, exp1.at(p, s))
                    pe.wait_ge(exp2.sem, exp2.at(p, max(s - 2, 0)))
                    turn_heads(turned, sm0[:, s % 2, :]).then_inc(turned1.sem, 1)
                u = s - 3
                if pos % 2 == 0 and 0 <= u < UA:
                    pe.wait_ge(exp1.sem, exp1.at(p, min(u + 3, UA)))
                    pe.wait_ge(less2.sem, less2.at(p, u + 1))
                    turn_heads(turned, dec0[:, u % 2, :]).then_inc(turned2.sem, 1)
                if pos % 2 == 1 and 0 <= u < UA:
                    b, j = divmod(u, 4)
                    pe.wait_ge(exp2.sem, exp2.at(p, u + 1))
                    if j == 0:
                        pe.wait_ge(att_ready.sem, att_ready.at(p, b))
                    for n_ in range(4):
                        hd = 8 * (n_ // 2) + 2 * j + n_ % 2
                        last = M.matmul(attn_out[:, hd * (DH0 + 1):(hd + 1) * (DH0 + 1)],
                                        e1[:, u % 2, n_ * P:(n_ + 1) * P], v0[:, b, hd, :], start=True, stop=True)
                    last.then_inc(weighed.sem, 1)

            def attention_sums(pos, p):
                u = pos // 2 - 1
                if pos % 2 == 0 and 0 <= u < UA:
                    pe.wait_ge(exp1.sem, exp1.at(p, u + 1))
                    if u == 0:
                        pe.wait_ge(v_ready.sem, v_ready.at(p, 1))
                    pe.wait_ge(distanced.sem, distanced.at(p, u))
                    for n_ in range(4):
                        last = M.matmul(sums[:, n_ * P:(n_ + 1) * P], e0[:, u % 2, n_ * P:(n_ + 1) * P], tri[:],
                                        start=True, stop=True)
                    last.then_inc(summed.sem, 1)

            def ffn_stage(pos, p):
                if pos == 1:
                    pe.wait_ge(attT_ready.sem, attT_ready.at(p, 1))
                    project_tokens(ffn, tokens(bT), wo0, PARTS).then_inc(wo_done.sem, 1)
                if pos == 0:
                    pe.wait_ge(att_ready.sem, att_ready.at(p, PAIR))
                    pe.wait_ge(xnT_ready.sem, xnT_ready.at(p - 1, 1))
                    turn(ffn, att).then_inc(att_turned.sem, 1)
                if pos == 4:
                    pe.wait_ge(xh1_ready.sem, xh1_ready.at(p, 1))
                    turn(ffn, s1).then_inc(x1_turned.sem, 1)
                if 5 <= pos < 9:
                    n_ = pos - 5
                    pe.wait_ge(x1T_ready.sem, x1T_ready.at(p, 1))
                    pe.wait_ge(relu_a.sem, relu_a.at(p, (n_ + 1) // 2))
                    pe.wait_ge(relu_v.sem, relu_v.at(p, n_ // 2))
                    for c in range(2):
                        last = product(ffn[:, c * T2:(c + 1) * T2],
                                       [(w1[i_][:, k, (2 * n_ + c) * P:(2 * n_ + c + 1) * P], bT[j_][:, k, :])
                                        for k in range(KC) for i_, j_ in PARTS])
                    last.then_inc(up_done.sem, 1)
                if pos in (9, 11):
                    b = (pos - 9) // 2
                    pe.wait_ge(relu_a.sem, relu_a.at(p, 2))
                    pe.wait_ge(relu_v.sem, relu_v.at(p, 2))
                    for k in range(FM):
                        last = M.matmul(ffn[:, b * D:(b + 1) * D], hT[:, k, b * P:(b + 1) * P], w2[:, k, :],
                                        start=(k == 0), stop=(k == FM - 1))
                    if b:
                        last.then_inc(down_done.sem, 1)
                if pos == 19:
                    pe.wait_ge(xn_ready.sem, xn_ready.at(p, 1))
                    turn(ffn, s1).then_inc(xn_turned.sem, 1)

            def mamba_stage(pos, p):
                if pos == 3:
                    pe.wait_ge(conv_in.sem, conv_in.at(p, 2))
                    product(mamba[1][0:DTR, 0:T2],
                            [(wdt[:, k, :], xnT[:, k, :]) for k in range(KC)]).then_inc(dt_done.sem, 1)
                if pos < 3:
                    lo, hi = CHUNKS[pos]
                    if pos == 0:
                        pe.wait_ge(xnT_ready.sem, xnT_ready.at(p, 1))
                        pe.wait_ge(yT_ready.sem, yT_ready.at(p - 1, PAIR))
                    elif pos == 1:
                        pe.wait_ge(h_ready.sem, h_ready.at(p - 1, 1))
                    else:
                        pe.wait_ge(conv_in.sem, conv_in.at(p, 1))
                    for n_, m in enumerate(range(lo, hi)):
                        last = product(mamba[pos % 2][:, n_ * T2:(n_ + 1) * T2],
                                       [(win[:, k, DI + m * P:DI + (m + 1) * P], xnT[:, k, :]) for k in range(KC)])
                    last.then_inc(xbc_done.sem, 1)
                if pos in (4, 5):
                    b = pos - 4
                    if b == 0:
                        pe.wait_ge(conv_in.sem, conv_in.at(p, 3))
                    else:
                        pe.wait_ge(dt_raw.sem, dt_raw.at(p, 1))
                    product(mamba[b][:], [(xnT[:, k, b * P:(b + 1) * P], win[:, k, 0:DI]) for k in range(KC)]).then_inc(z_done.sem, 1)
                if pos in (8, 9, 11, 12):
                    n_ = (8, 9, 11, 12).index(pos)
                    pe.wait_ge(decay_parts.sem, decay_parts.at(p, 1))
                    if pos in (8, 9):
                        pe.wait_ge(z_exp.sem, z_exp.at(p, pos - 7))
                    elif pos == 11:
                        pe.wait_ge(scanned.sem, scanned.at(p, 2))
                    else:
                        pe.wait_ge(cb_ready.sem, cb_ready.at(p, 1))
                    for m in range(4):
                        hd = 4 * (n_ % 2) + m
                        last = M.matmul(mamba[MB[pos]][:, m * P:(m + 1) * P], sel[:, hd:hd + 1].broadcast_to([DTR, P]),
                                        decay_p[:, n_ // 2, :], start=True, stop=True)
                    last.then_inc(spread.sem, 1)
                if pos == 10:
                    pe.wait_ge(xc_ready.sem, xc_ready.at(p, 1))
                    pe.wait_ge(scanned.sem, scanned.at(p, 1))
                    pe.wait_ge(sp_ready.sem, sp_ready.at(p, 1))
                    for b in range(PAIR):
                        M.matmul(mamba[0][:, b * P:(b + 1) * P], xc[:, 4, b * P:(b + 1) * P],
                                 xc[:, 5, b * P:(b + 1) * P], start=True, stop=True)
                    for b in range(PAIR):
                        last = M.transpose(mamba[0][:, 2 * P + b * HM:2 * P + (b + 1) * HM], sp[0:HM, b * P:(b + 1) * P],
                                           ident[0:HM, 0:HM])
                    last.then_inc(cb_done.sem, 1)
                if pos in (14, 15):
                    b = pos - 14
                    pe.wait_ge(xc_ready.sem, xc_ready.at(p, 3))
                    pe.wait_ge(scanned.sem, scanned.at(p, 3 + b))
                    for c in range(DI // P):
                        last = M.transpose(mamba[MB[pos]][:, c * P:(c + 1) * P], xc[:, c, b * P:(b + 1) * P], ident[:])
                    last.then_inc(x_turned.sem, 1)
                if pos in (16, 17):
                    b = pos - 16
                    pe.wait_ge(mixed.sem, mixed.at(p, b + 1))
                    pe.wait_ge(xtok.sem, xtok.at(p, b + 1))
                    for n_ in range(HM):
                        last = M.matmul(mamba[MB[pos]][:, n_ * HD:(n_ + 1) * HD], g[:, b, n_ * P:(n_ + 1) * P],
                                        dtx[:, b, n_ * HD:(n_ + 1) * HD], start=True, stop=True)
                    last.then_inc(y_done.sem, 1)
                if pos in (18, 19):
                    b = pos - 18
                    pe.wait_ge(y_gated.sem, y_gated.at(p, b + 1))
                    for c in range(DI // P):
                        last = M.transpose(mamba[(b + 1) % 2][:, c * P:(c + 1) * P], y[:, b, c * P:(c + 1) * P], ident[:])
                    last.then_inc(y_turned.sem, 1)
                if pos == 21:
                    pe.wait_ge(yT_ready.sem, yT_ready.at(p, PAIR))
                    project_tokens(mamba[1], lambda i_, k, b: yT[:, b, k * P:(k + 1) * P], [wout],
                                   chunks=DI // P).then_inc(mout_done.sem, 1)

            def cross_stage(pos, p):
                if pos == 0:
                    pe.wait_ge(c_loaded.sem, c_loaded.at(p, 16))
                    pe.wait_ge(out_ready.sem, out_ready.at(p - 1, 1))
                    project(cross, [wk1], [cTc]).then_inc(k1_proj.sem, 1)
                if pos == 1:
                    pe.wait_ge(k1_ready.sem, k1_ready.at(p, 1))
                    project_tokens(cross, tokens([cTc]), [wv1]).then_inc(v1_proj.sem, 1)
                if pos == 3:
                    pe.wait_ge(xh3_ready.sem, xh3_ready.at(p, 1))
                    pe.wait_ge(v1_ready.sem, v1_ready.at(p, 1))
                    turn(cross, h).then_inc(xh3_turned.sem, 1)
                if pos == 4:
                    pe.wait_ge(xh3T_ready.sem, xh3T_ready.at(p, 1))
                    project(cross, wq1, hT1, PARTS).then_inc(q1_proj.sem, 1)
                v, r = divmod(pos - 6, 3)
                if pos >= 6 and r == 0 and v < UC:
                    if v == 0:
                        pe.wait_ge(q1_ready.sem, q1_ready.at(p, 1))
                    pe.wait_ge(exp3.sem, exp3.at(p, v))
                    pe.wait_ge(co_ready.sem, co_ready.at(p, max(v - 1, 0)))
                    score(cross, q1, k1, 64 * (v % 2), 64, v // 2).then_inc(scored3.sem, 1)
                if pos >= 6 and r == 2 and v < UC:
                    pe.wait_ge(less3.sem, less3.at(p, v + 1))
                    pe.wait_ge(co_ready.sem, co_ready.at(p, v))
                    turn_heads(cross, sc3[:, 0, :]).then_inc(turned3.sem, 1)
                v, r = divmod(pos - 10, 3)
                if pos >= 10 and r == 0 and v < UC:
                    b, jj = divmod(v, 2)
                    pe.wait_ge(exp3.sem, exp3.at(p, v + 1))
                    pe.wait_ge(taken3.sem, taken3.at(p, min(v + 2, UC)))
                    for n_ in range(4):
                        hd = 4 * (n_ // 2) + 2 * jj + n_ % 2
                        last = M.matmul(cross[:, n_ * (DH1 + 1):(n_ + 1) * (DH1 + 1)],
                                        e3[:, 0, n_ * P:(n_ + 1) * P], v1[:, b, hd, :], start=True, stop=True)
                    last.then_inc(weighed3.sem, 1)
                if pos == 20:
                    pe.wait_ge(co_ready.sem, co_ready.at(p, UC))
                    turn(cross, co).then_inc(co_turned.sem, 1)
                if pos == 21:
                    pe.wait_ge(coT_ready.sem, coT_ready.at(p, 1))
                    project_tokens(cross, tokens(hT1), wo1, PARTS).then_inc(out_proj.sem, 1)

            def body(i, on, set_up_rest={}):
                for pos in range(POS):
                    if pos in set_up_rest:
                        set_up_rest[pos]()
                    if on[1]:
                        ffn_stage(pos, i - 1)
                    if on[0]:
                        attention_scores(pos, i)
                    if on[2]:
                        mamba_stage(pos, i - 2)
                    if on[3]:
                        cross_stage(pos, i - 3)
                    if on[0]:
                        attention_turns(pos, i)
                    if on[0]:
                        attention_sums(pos, i)
                    if on[4]:
                        queries_keys(pos, i + 1)
            run(pe, body, {8: set_up_query_bias, 11: lambda: set_up_ffn_bias(0, 4), 13: lambda: set_up_ffn_bias(4, FM),
                          POS - 1: see_set_up})


MB = {8: 0, 9: 1, 11: 1, 12: 0, 14: 1, 15: 0, 16: 1, 17: 0}
SETUP_A = 1 + 3 + 3 + 2 * KC
SETUP_TENSOR = SETUP_A + 1 + 5 + KC * 7 + 4
SETUP_DONE = SETUP_TENSOR + 1 + 2 * KC + 1 + KC * 6


def layouts(inputs):
    import numpy as np

    def arr(n):
        return np.ascontiguousarray(np.asarray(inputs[n]))

    def chunked(w):
        return np.ascontiguousarray(w.reshape(-1, P, w.shape[1]).transpose(1, 0, 2))

    def column(v):
        return np.ascontiguousarray(v.reshape(-1, P).T)

    x, c = arr("x"), arr("ctx_1024")
    q, k = np.arange(P)[:, None], np.arange(P)[None, :]
    tri = (q > k).astype(np.float32)
    tri[:, P - 1] = 1.0
    f = np.float32
    sel = np.zeros((DTR, HM), f)
    sel[0:HM] = sel[32:DTR] = np.eye(HM, dtype=f)
    par = (np.arange(P) // DH0) % 2
    par1 = (np.arange(P) // DH1) % 2
    d = {
        "xT": np.ascontiguousarray(x.reshape(-1, D).T), "cT": np.ascontiguousarray(c.reshape(-1, D).T),
        "x": np.ascontiguousarray(x.transpose(1, 0, 2)),
        "mask": arr("mask_1xS2_bf0").reshape(P),
        "ident": np.eye(P, dtype=f), "tri": tri,
        "later": np.where(k > q, -1e32, 0.0).astype(f),
        "eye4": np.tile(np.eye(P, dtype=f), (1, 4)), "dist": np.maximum(q - k, 0).astype(f), "sel": sel,
        "half16": (np.stack([1 - par, par], 1) / np.sqrt(DH0)).astype(f),
        "half32": (np.stack([1 - par1, par1], 1) / np.sqrt(DH1)).astype(f),
    }
    for name, src in (("wk0", "L0_xattn_Wk"), ("wv0", "L0_xattn_Wv"), ("wo0", "L0_xattn_Wo"),
                      ("w1", "L0_xattn_W1"), ("w2", "L0_xattn_W2")):
        d[name] = chunked(arr(src).T)
    for name, src in (("win", "in_proj_w"), ("wout", "out_proj_w"), ("wq1", "Wq"), ("wk1", "Wk"),
                      ("wv1", "Wv"), ("wo1", "Wo")):
        d[name] = chunked(arr("L1_xattn_" + src))
    for name, src in (("bk0", "L0_xattn_bk"), ("b1", "L0_xattn_b1"), ("ln1_w", "L0_xattn_ln1_w"),
                      ("ln1_b", "L0_xattn_ln1_b"), ("m_norm_w", "L1_xattn_m_norm_w"), ("gnorm_w", "L1_xattn_gnorm_w"),
                      ("ca_ln_w", "L1_xattn_ca_ln_w"), ("ca_ln_b", "L1_xattn_ca_ln_b"), ("conv_b", "L1_xattn_conv_b")):
        d[name] = column(arr(src))
    d["conv_w"] = chunked(arr("L1_xattn_conv_w"))
    for name in ("dt_bias", "A_log"):
        d[name] = np.zeros((DTR, 1), f)
        d[name][0:HM, 0] = d[name][32:DTR, 0] = arr("L1_xattn_" + name)
    for name, src in (("bv0", "L0_xattn_bv"), ("bo0", "L0_xattn_bo"), ("b2", "L0_xattn_b2"),
                      ("ln1_w_row", "L0_xattn_ln1_w"), ("ln1_b_row", "L0_xattn_ln1_b"),
                      ("ln2_w_row", "L0_xattn_ln2_w"), ("ln2_b_row", "L0_xattn_ln2_b"), ("D_skip", "L1_xattn_D_skip"),
                      ("gammas", "L0_xattn_gammas")):
        d[name] = arr(src).reshape(-1)
    return d


def kernel(**inputs):
    import numpy as np
    import concourse.bacc as bacc
    from concourse.bass_utils import run_bass_kernel_spmd

    arrays = layouts(inputs)
    nseq = arrays["x"].shape[1]
    nc = bacc.Bacc("TRN2", target_bir_lowering=False, num_devices=1)
    aps = {n: nc.dram_tensor("in_" + n, v.shape, mybir.dt.from_np(v.dtype), kind="ExternalInput").ap()
           for n, v in arrays.items()}
    out = nc.dram_tensor("out", [nseq, P, D], F32, kind="ExternalOutput").ap()
    build(nc, aps, out.rearrange("n t d -> t n d"))
    r = run_bass_kernel_spmd(nc, [{"in_" + n: v for n, v in arrays.items()}], core_ids=[0])
    return np.asarray(r.results[0]["out"])
```
